# Optimizing a Trainium2 kernel written in Bass

```python
import numpy as np
import jax
import jax.numpy as jnp

def _softmax(x, axis=-1):
    return jax.nn.softmax(x, axis=axis)

def _gelu(x):
    return jax.nn.gelu(x, approximate=True)

def _silu(x):
    return jax.nn.silu(x)

def _sigmoid(x):
    return jax.nn.sigmoid(x)

def _layernorm(x, axis=-1, eps=1e-05):
    m = jnp.mean(x, axis=axis, keepdims=True)
    v = jnp.var(x, axis=axis, keepdims=True)
    return (x - m) / jnp.sqrt(v + eps)

def _scatter_add(tgt, idx, src, axis=0):
    return tgt.at[idx].add(src)

def _segment_sum(src, seg, n):
    return jax.ops.segment_sum(src, seg, n)
kernel_name = 'mk_decoder_postln_d2_seqx_r8_f0cf16'

def setup_inputs(seed: int=0):
    np.random.seed(seed)
    _w = jnp.asarray

    def _rec_inputs():
        import jax
        import jax.numpy as jnp
        _rk = jax.random.key(seed)
        x = 7.22e-05 + 1 * jax.random.normal(jax.random.fold_in(_rk, 1), (128, 64, 128), jnp.float32)
        _lenS = 64 - jax.random.randint(jax.random.fold_in(_rk, 7), (128,), 0, max(1, 64 // 4) + 1, jnp.int32)
        _lenS2 = 64 - jax.random.randint(jax.random.fold_in(_rk, 8), (128,), 0, max(1, 64 // 4) + 1, jnp.int32)
        _ctx_1024P = jax.random.normal(jax.random.fold_in(_rk, 11), (128, 16, 128), jnp.float32)
        _ctx_1024c = jax.random.dirichlet(jax.random.fold_in(_rk, 511), 0.3 * jnp.ones((16,), jnp.float32), (128, 64))
        _ctx_1024t = jnp.einsum('bsk,bkd->bsd', _ctx_1024c, _ctx_1024P)
        _ctx_1024t = _ctx_1024t * jax.lax.rsqrt(jnp.mean(jnp.square(_ctx_1024t)) + 1e-12) * 0.953939
        ctx_1024 = -0.000514642 + 1.00011 * (_ctx_1024t + 0.3 * jax.random.normal(jax.random.fold_in(_rk, 611), (128, 64, 128), jnp.float32))
        return (x, ctx_1024)
    x, ctx_1024 = _rec_inputs()

    def _L0_attn_setup():
        import jax, jax.numpy as jnp
        import numpy as np
        B, N, D = (4, 512, 128)
        H, DH = (16, 64)
        DFF = 512
        M = 64
        EPS_KERN = 1e-06
        EPS_LN = 1e-06

        def _softmax_kernel_feats(data, proj, is_query):
            dn = 1.0 / jnp.sqrt(jnp.sqrt(jnp.float32(data.shape[-1])))
            ratio = 1.0 / jnp.sqrt(jnp.float32(proj.shape[0]))
            data_dash = jnp.einsum('bnhd,md->bnhm', data * dn, proj)
            diag = jnp.sum(jnp.square(data), axis=-1, keepdims=True) * (dn * dn) / 2.0
            if is_query:
                mx = jnp.max(data_dash, axis=-1, keepdims=True)
            else:
                mx = jnp.max(data_dash)
            return ratio * (jnp.exp(data_dash - diag - mx) + EPS_KERN)

        def _layernorm(x, g, b):
            mu = jnp.mean(x, axis=-1, keepdims=True)
            var = jnp.mean(jnp.square(x - mu), axis=-1, keepdims=True)
            return (x - mu) * jax.lax.rsqrt(var + EPS_LN) * g + b

        def _encoder_forward(x, Wq, Wk, Wv, Wo, proj, W1, b1, W2, b2, ln1_g, ln1_b, ln2_g, ln2_b):
            q = jnp.einsum('bnd,dhk->bnhk', x, Wq)
            k = jnp.einsum('bnd,dhk->bnhk', x, Wk)
            v = jnp.einsum('bnd,dhk->bnhk', x, Wv)
            qf = _softmax_kernel_feats(q, proj, True)
            kf = _softmax_kernel_feats(k, proj, False)
            kv = jnp.einsum('bnhm,bnhd->bhmd', kf, v)
            num = jnp.einsum('bnhm,bhmd->bnhd', qf, kv)
            den = jnp.einsum('bnhm,bhm->bnh', qf, jnp.sum(kf, axis=1))
            attn = num / den[..., None]
            attn_out = jnp.einsum('bnhd,hdo->bno', attn, Wo)
            out1 = _layernorm(x + attn_out, ln1_g, ln1_b)
            h = jax.nn.elu(out1 @ W1 + b1)
            ffn_out = h @ W2 + b2
            return _layernorm(out1 + ffn_out, ln2_g, ln2_b)
        key = jax.random.key(seed)
        ks = jax.random.split(key, 12)
        s = 0.02
        inp = {'x': jax.random.normal(ks[0], (B, N, D), jnp.float32), 'Wq': jax.random.normal(ks[1], (D, H, DH), jnp.float32) * s, 'Wk': jax.random.normal(ks[2], (D, H, DH), jnp.float32) * s, 'Wv': jax.random.normal(ks[3], (D, H, DH), jnp.float32) * s, 'Wo': jax.random.normal(ks[4], (H, DH, D), jnp.float32) * s, 'proj': jax.random.normal(ks[5], (M, DH), jnp.float32), 'W1': jax.random.normal(ks[6], (D, DFF), jnp.float32) * s, 'b1': jnp.zeros((DFF,), jnp.float32), 'W2': jax.random.normal(ks[7], (DFF, D), jnp.float32) * s, 'b2': jnp.zeros((D,), jnp.float32), 'ln1_g': jnp.ones((D,), jnp.float32), 'ln1_b': jnp.zeros((D,), jnp.float32), 'ln2_g': jnp.ones((D,), jnp.float32), 'ln2_b': jnp.zeros((D,), jnp.float32)}
        return inp
    _L0_attn_all = _L0_attn_setup()
    _L0_attn_in = {k: v for k, v in _L0_attn_all.items() if k in ('Wq', 'Wk', 'Wv', 'Wo', 'proj', 'W1', 'b1', 'W2', 'b2', 'ln1_g', 'ln1_b', 'ln2_g', 'ln2_b')}
    del _L0_attn_all

    def _L0_xattn_setup():
        import jax, jax.numpy as jnp
        import numpy as np
        B, L_ENC, L_DEC, D = (16, 64, 128, 128)
        key = jax.random.key(seed)
        k1, k2, k3, k4, k5, k6 = jax.random.split(key, 6)
        encoder_hc = jax.random.normal(k1, (B, L_ENC, D), dtype=jnp.float32)
        decoder_hq = jax.random.normal(k2, (B, L_DEC, D), dtype=jnp.float32)
        w_sim = jax.random.normal(k3, (3 * D,), dtype=jnp.float32) * 0.02
        b_sim = jax.random.normal(k4, (1,), dtype=jnp.float32) * 0.02
        W_qv = jax.random.normal(k5, (4 * D, D), dtype=jnp.float32) * 0.02
        b_qv = jax.random.normal(k6, (D,), dtype=jnp.float32) * 0.02
        return {'encoder_hc': encoder_hc, 'decoder_hq': decoder_hq, 'w_sim': w_sim, 'b_sim': b_sim, 'W_qv': W_qv, 'b_qv': b_qv}
    _L0_xattn_all = _L0_xattn_setup()
    _L0_xattn_in = {k: v for k, v in _L0_xattn_all.items() if k in ('w_sim', 'b_sim', 'W_qv', 'b_qv')}
    del _L0_xattn_all

    def _L0_ffn_setup():
        import jax, jax.numpy as jnp
        import numpy as np
        IN_F = 128
        OUT_F = 128
        B, S = (8, 512)

        def _pack_ternary(tern):
            enc = (tern + 1.0).astype(jnp.int32).reshape(-1)
            return (enc[0::4] | enc[1::4] << 2 | enc[2::4] << 4 | enc[3::4] << 6).astype(jnp.int32)
        key = jax.random.key(seed)
        kx, kw = jax.random.split(key)
        x = jax.random.normal(kx, (B, S, IN_F), dtype=jnp.float32)
        w = jax.random.normal(kw, (OUT_F, IN_F), dtype=jnp.float32) * 0.02
        scale = jnp.maximum(jnp.mean(jnp.abs(w)), 1e-05)
        wn = w / scale
        tern = jnp.sign(wn) * (jnp.abs(wn) > 0.5).astype(jnp.float32)
        packed = _pack_ternary(tern)
        bias = jnp.zeros((OUT_F,), dtype=jnp.float32)
        return {'x': x, 'packed_weight': packed, 'weight_scale': scale.reshape(1), 'bias': bias}
    _L0_ffn_all = _L0_ffn_setup()
    _L0_ffn_in = {k: v for k, v in _L0_ffn_all.items() if k in ('packed_weight', 'weight_scale', 'bias')}
    del _L0_ffn_all

    def _L1_attn_setup():
        import jax, jax.numpy as jnp
        import numpy as np
        import math
        NUM_HEADS = 16
        NUM_BUCKETS = 32
        MAX_DISTANCE = 128
        ALPHA = 32.0

        def _rel_bucket(rel_pos):
            nb = NUM_BUCKETS // 2
            buckets = (rel_pos > 0).astype(jnp.int32) * nb
            rel_pos = jnp.abs(rel_pos)
            max_exact = nb // 2
            is_small = rel_pos < max_exact
            large = max_exact + (jnp.log(rel_pos.astype(jnp.float32) / max_exact + 1e-06) / math.log(MAX_DISTANCE / max_exact) * (nb - max_exact)).astype(jnp.int32)
            large = jnp.minimum(large, nb - 1)
            return buckets + jnp.where(is_small, rel_pos, large)
        key = jax.random.key(seed)
        ks = jax.random.split(key, 12)
        T, B, E = (128, 4, 128)
        hd = E // NUM_HEADS
        s = 0.02
        f32 = jnp.float32
        return {'query': jax.random.normal(ks[0], (T, B, E), f32), 'q_w': jax.random.normal(ks[1], (E, E), f32) * s, 'q_b': jnp.zeros((E,), f32), 'k_w': jax.random.normal(ks[2], (E, E), f32) * s, 'k_b': jnp.zeros((E,), f32), 'v_w': jax.random.normal(ks[3], (E, E), f32) * s, 'v_b': jnp.zeros((E,), f32), 'out_w': jax.random.normal(ks[4], (E, E), f32) * s, 'out_b': jnp.zeros((E,), f32), 'rel_emb': jax.random.normal(ks[5], (NUM_BUCKETS, NUM_HEADS), f32) * 0.1, 'grep_w': jax.random.normal(ks[6], (hd, 8), f32) * s, 'grep_b': jnp.zeros((8,), f32), 'grep_a': jnp.ones((1, NUM_HEADS, 1, 1), f32), 'bias_k': jax.random.normal(ks[7], (1, 1, E), f32) * s, 'bias_v': jax.random.normal(ks[8], (1, 1, E), f32) * s}
    _L1_attn_all = _L1_attn_setup()
    _L1_attn_in = {k: v for k, v in _L1_attn_all.items() if k in ('q_w', 'q_b', 'k_w', 'k_b', 'v_w', 'v_b', 'out_w', 'out_b', 'rel_emb', 'grep_w', 'grep_b', 'grep_a', 'bias_k', 'bias_v')}
    del _L1_attn_all

    def _L1_xattn_setup():
        import jax, jax.numpy as jnp
        import numpy as np
        DIM = 128
        N_HEADS = 16
        HEAD_DIM = DIM // N_HEADS
        B, L, M = (2, 256, 256)
        key = jax.random.key(seed)
        ks = jax.random.split(key, 7)
        s = 1.0 / np.sqrt(DIM)
        return {'q': jax.random.normal(ks[0], (B, L, DIM), dtype=jnp.float32), 'k': jax.random.normal(ks[1], (B, M, DIM), dtype=jnp.float32), 'v': jax.random.normal(ks[2], (B, M, DIM), dtype=jnp.float32), 'Wq': jax.random.normal(ks[3], (DIM, DIM), dtype=jnp.float32) * s, 'Wk': jax.random.normal(ks[4], (DIM, DIM), dtype=jnp.float32) * s, 'Wv': jax.random.normal(ks[5], (DIM, DIM), dtype=jnp.float32) * s, 'Wo': jax.random.normal(ks[6], (DIM, DIM), dtype=jnp.float32) * s}
    _L1_xattn_all = _L1_xattn_setup()
    _L1_xattn_in = {k: v for k, v in _L1_xattn_all.items() if k in ('Wq', 'Wk', 'Wv', 'Wo')}
    del _L1_xattn_all

    def _L1_ffn_setup():
        import jax, jax.numpy as jnp
        import numpy as np
        H = 128
        I = 64
        E = 64
        G = 8
        TOPK_GROUP = 4
        K = 8
        I_SH = 128
        SCALE = 2.5

        def _route(x, router_w, e_bias):
            T = x.shape[0]
            scores = jax.nn.sigmoid(x.astype(jnp.float32) @ router_w.T.astype(jnp.float32))
            sfc = jax.lax.stop_gradient(scores) + e_bias[None, :]
            group_scores = jax.lax.top_k(sfc.reshape(T, G, E // G), 2)[0].sum(-1)
            _, gidx = jax.lax.top_k(group_scores, TOPK_GROUP)
            gmask = jax.nn.one_hot(gidx, G, dtype=sfc.dtype).sum(1)
            smask = jnp.repeat(gmask, E // G, axis=1)
            masked = jnp.where(smask > 0, sfc, 0.0)
            _, topk_idx = jax.lax.top_k(masked, K)
            w = jnp.take_along_axis(scores, topk_idx, axis=1)
            w = w / (w.sum(-1, keepdims=True) + 1e-20)
            return (topk_idx, w * SCALE)
        key = jax.random.key(seed)
        ks = jax.random.split(key, 9)
        s = 0.02
        return {'hidden_states': jax.random.normal(ks[0], (2, 128, H), jnp.float32), 'router_w': jax.random.normal(ks[1], (E, H), jnp.float32) * s, 'e_bias': jnp.zeros((E,), jnp.float32), 'Wg': jax.random.normal(ks[2], (E, H, I), jnp.float32) * s, 'Wu': jax.random.normal(ks[3], (E, H, I), jnp.float32) * s, 'Wd': jax.random.normal(ks[4], (E, I, H), jnp.float32) * s, 'SWg': jax.random.normal(ks[5], (H, I_SH), jnp.float32) * s, 'SWu': jax.random.normal(ks[6], (H, I_SH), jnp.float32) * s, 'SWd': jax.random.normal(ks[7], (I_SH, H), jnp.float32) * s}
    _L1_ffn_all = _L1_ffn_setup()
    _L1_ffn_in = {k: v for k, v in _L1_ffn_all.items() if k in ('router_w', 'e_bias', 'Wg', 'Wu', 'Wd', 'SWg', 'SWu', 'SWd')}
    del _L1_ffn_all
    return {'x': x, 'ctx_1024': ctx_1024, 'L0_attn_Wq': _L0_attn_in['Wq'], 'L0_attn_Wk': _L0_attn_in['Wk'], 'L0_attn_Wv': _L0_attn_in['Wv'], 'L0_attn_Wo': _L0_attn_in['Wo'], 'L0_attn_proj': _L0_attn_in['proj'], 'L0_attn_W1': _L0_attn_in['W1'], 'L0_attn_b1': _L0_attn_in['b1'], 'L0_attn_W2': _L0_attn_in['W2'], 'L0_attn_b2': _L0_attn_in['b2'], 'L0_attn_ln1_g': _L0_attn_in['ln1_g'], 'L0_attn_ln1_b': _L0_attn_in['ln1_b'], 'L0_attn_ln2_g': _L0_attn_in['ln2_g'], 'L0_attn_ln2_b': _L0_attn_in['ln2_b'], 'L0_xattn_w_sim': _L0_xattn_in['w_sim'], 'L0_xattn_b_sim': _L0_xattn_in['b_sim'], 'L0_xattn_W_qv': _L0_xattn_in['W_qv'], 'L0_xattn_b_qv': _L0_xattn_in['b_qv'], 'L0_ffn_packed_weight': _L0_ffn_in['packed_weight'], 'L0_ffn_weight_scale': _L0_ffn_in['weight_scale'], 'L0_ffn_bias': _L0_ffn_in['bias'], 'L1_attn_q_w': _L1_attn_in['q_w'], 'L1_attn_q_b': _L1_attn_in['q_b'], 'L1_attn_k_w': _L1_attn_in['k_w'], 'L1_attn_k_b': _L1_attn_in['k_b'], 'L1_attn_v_w': _L1_attn_in['v_w'], 'L1_attn_v_b': _L1_attn_in['v_b'], 'L1_attn_out_w': _L1_attn_in['out_w'], 'L1_attn_out_b': _L1_attn_in['out_b'], 'L1_attn_rel_emb': _L1_attn_in['rel_emb'], 'L1_attn_grep_w': _L1_attn_in['grep_w'], 'L1_attn_grep_b': _L1_attn_in['grep_b'], 'L1_attn_grep_a': _L1_attn_in['grep_a'], 'L1_attn_bias_k': _L1_attn_in['bias_k'], 'L1_attn_bias_v': _L1_attn_in['bias_v'], 'L1_xattn_Wq': _L1_xattn_in['Wq'], 'L1_xattn_Wk': _L1_xattn_in['Wk'], 'L1_xattn_Wv': _L1_xattn_in['Wv'], 'L1_xattn_Wo': _L1_xattn_in['Wo'], 'L1_ffn_router_w': _L1_ffn_in['router_w'], 'L1_ffn_e_bias': _L1_ffn_in['e_bias'], 'L1_ffn_Wg': _L1_ffn_in['Wg'], 'L1_ffn_Wu': _L1_ffn_in['Wu'], 'L1_ffn_Wd': _L1_ffn_in['Wd'], 'L1_ffn_SWg': _L1_ffn_in['SWg'], 'L1_ffn_SWu': _L1_ffn_in['SWu'], 'L1_ffn_SWd': _L1_ffn_in['SWd']}

def reference(x, ctx_1024, L0_attn_Wq, L0_attn_Wk, L0_attn_Wv, L0_attn_Wo, L0_attn_proj, L0_attn_W1, L0_attn_b1, L0_attn_W2, L0_attn_b2, L0_attn_ln1_g, L0_attn_ln1_b, L0_attn_ln2_g, L0_attn_ln2_b, L0_xattn_w_sim, L0_xattn_b_sim, L0_xattn_W_qv, L0_xattn_b_qv, L0_ffn_packed_weight, L0_ffn_weight_scale, L0_ffn_bias, L1_attn_q_w, L1_attn_q_b, L1_attn_k_w, L1_attn_k_b, L1_attn_v_w, L1_attn_v_b, L1_attn_out_w, L1_attn_out_b, L1_attn_rel_emb, L1_attn_grep_w, L1_attn_grep_b, L1_attn_grep_a, L1_attn_bias_k, L1_attn_bias_v, L1_xattn_Wq, L1_xattn_Wk, L1_xattn_Wv, L1_xattn_Wo, L1_ffn_router_w, L1_ffn_e_bias, L1_ffn_Wg, L1_ffn_Wu, L1_ffn_Wd, L1_ffn_SWg, L1_ffn_SWu, L1_ffn_SWd):
    import jax
    import jax.numpy as jnp

    def _L0_attn_ref(x, Wq, Wk, Wv, Wo, proj, W1, b1, W2, b2, ln1_g, ln1_b, ln2_g, ln2_b):
        import jax, jax.numpy as jnp
        import numpy as np
        B, N, D = (4, 512, 128)
        H, DH = (16, 64)
        DFF = 512
        M = 64
        EPS_KERN = 1e-06
        EPS_LN = 1e-06

        def _softmax_kernel_feats(data, proj, is_query):
            dn = 1.0 / jnp.sqrt(jnp.sqrt(jnp.float32(data.shape[-1])))
            ratio = 1.0 / jnp.sqrt(jnp.float32(proj.shape[0]))
            data_dash = jnp.einsum('bnhd,md->bnhm', data * dn, proj)
            diag = jnp.sum(jnp.square(data), axis=-1, keepdims=True) * (dn * dn) / 2.0
            if is_query:
                mx = jnp.max(data_dash, axis=-1, keepdims=True)
            else:
                mx = jnp.max(data_dash)
            return ratio * (jnp.exp(data_dash - diag - mx) + EPS_KERN)

        def _layernorm(x, g, b):
            mu = jnp.mean(x, axis=-1, keepdims=True)
            var = jnp.mean(jnp.square(x - mu), axis=-1, keepdims=True)
            return (x - mu) * jax.lax.rsqrt(var + EPS_LN) * g + b

        def _encoder_forward(x, Wq, Wk, Wv, Wo, proj, W1, b1, W2, b2, ln1_g, ln1_b, ln2_g, ln2_b):
            q = jnp.einsum('bnd,dhk->bnhk', x, Wq)
            k = jnp.einsum('bnd,dhk->bnhk', x, Wk)
            v = jnp.einsum('bnd,dhk->bnhk', x, Wv)
            qf = _softmax_kernel_feats(q, proj, True)
            kf = _softmax_kernel_feats(k, proj, False)
            kv = jnp.einsum('bnhm,bnhd->bhmd', kf, v)
            num = jnp.einsum('bnhm,bhmd->bnhd', qf, kv)
            den = jnp.einsum('bnhm,bhm->bnh', qf, jnp.sum(kf, axis=1))
            attn = num / den[..., None]
            attn_out = jnp.einsum('bnhd,hdo->bno', attn, Wo)
            out1 = _layernorm(x + attn_out, ln1_g, ln1_b)
            h = jax.nn.elu(out1 @ W1 + b1)
            ffn_out = h @ W2 + b2
            return _layernorm(out1 + ffn_out, ln2_g, ln2_b)
        return _encoder_forward(x, Wq, Wk, Wv, Wo, proj, W1, b1, W2, b2, ln1_g, ln1_b, ln2_g, ln2_b)

    def _L0_xattn_ref(encoder_hc, decoder_hq, w_sim, b_sim, W_qv, b_qv):
        import jax, jax.numpy as jnp
        import numpy as np
        B, L_ENC, L_DEC, D = (16, 64, 128, 128)
        d = encoder_hc.shape[-1]
        w1, w2, w3 = (w_sim[:d], w_sim[d:2 * d], w_sim[2 * d:])
        Sim = (encoder_hc @ w1)[:, :, None] + (decoder_hq @ w2)[:, None, :] + jnp.einsum('bid,bjd->bij', encoder_hc * w3, decoder_hq) + b_sim[0]
        A = jax.nn.softmax(Sim, axis=2)
        hq_hat = jnp.einsum('bij,bjd->bid', A, decoder_hq)
        Batt = jax.nn.softmax(jnp.max(Sim, axis=2), axis=1)
        hc_bar = jnp.einsum('bi,bid->bd', Batt, encoder_hc)[:, None, :]
        hc_hat = jnp.broadcast_to(hc_bar, encoder_hc.shape)
        feats = jnp.concatenate([encoder_hc, hq_hat, encoder_hc * hq_hat, encoder_hc * hc_hat], axis=-1)
        hcq = feats @ W_qv + b_qv
        return hcq

    def _L0_ffn_ref(x, packed_weight, weight_scale, bias):
        import jax, jax.numpy as jnp
        import numpy as np
        IN_F = 128
        OUT_F = 128
        B, S = (8, 512)

        def _pack_ternary(tern):
            enc = (tern + 1.0).astype(jnp.int32).reshape(-1)
            return (enc[0::4] | enc[1::4] << 2 | enc[2::4] << 4 | enc[3::4] << 6).astype(jnp.int32)
        n = OUT_F * IN_F
        shifts = jnp.array([0, 2, 4, 6], dtype=jnp.int32)
        enc = (packed_weight[None, :] >> shifts[:, None] & 3).reshape(-1)[:n]
        w = (enc.astype(jnp.float32) - 1.0).reshape(OUT_F, IN_F) * weight_scale
        act_scale = 127.0 / jnp.maximum(jnp.max(jnp.abs(x), axis=-1, keepdims=True), 1e-05)
        x_dq = jnp.clip(jnp.round(x * act_scale), -128.0, 127.0) / act_scale
        return jnp.einsum('bsi,oi->bso', x_dq, w) + bias

    def _L1_attn_ref(query, q_w, q_b, k_w, k_b, v_w, v_b, out_w, out_b, rel_emb, grep_w, grep_b, grep_a, bias_k, bias_v):
        import jax, jax.numpy as jnp
        import numpy as np
        import math
        NUM_HEADS = 16
        NUM_BUCKETS = 32
        MAX_DISTANCE = 128
        ALPHA = 32.0

        def _rel_bucket(rel_pos):
            nb = NUM_BUCKETS // 2
            buckets = (rel_pos > 0).astype(jnp.int32) * nb
            rel_pos = jnp.abs(rel_pos)
            max_exact = nb // 2
            is_small = rel_pos < max_exact
            large = max_exact + (jnp.log(rel_pos.astype(jnp.float32) / max_exact + 1e-06) / math.log(MAX_DISTANCE / max_exact) * (nb - max_exact)).astype(jnp.int32)
            large = jnp.minimum(large, nb - 1)
            return buckets + jnp.where(is_small, rel_pos, large)
        tgt_len, bsz, embed_dim = query.shape
        nh = NUM_HEADS
        hd = embed_dim // nh
        scaling = hd ** (-0.5)
        q = query @ q_w + q_b
        k = query @ k_w + k_b
        v = query @ v_w + v_b
        q = q * scaling / ALPHA
        k = jnp.concatenate([k, jnp.tile(bias_k, (1, bsz, 1))], axis=0)
        v = jnp.concatenate([v, jnp.tile(bias_v, (1, bsz, 1))], axis=0)
        q = jnp.transpose(q.reshape(tgt_len, bsz, nh, hd), (1, 0, 2, 3)).reshape(bsz * nh, tgt_len, hd)
        k = jnp.transpose(k.reshape(-1, bsz, nh, hd), (1, 0, 2, 3)).reshape(bsz * nh, -1, hd)
        v = jnp.transpose(v.reshape(-1, bsz, nh, hd), (1, 0, 2, 3)).reshape(bsz * nh, -1, hd)
        src_len = k.shape[1]
        attn_weights = jnp.einsum('bth,bsh->bts', q, k)
        rel_pos = jnp.arange(src_len)[None, :] - jnp.arange(tgt_len)[:, None]
        buckets = _rel_bucket(rel_pos)
        pb = rel_emb[buckets]
        pb = jnp.transpose(pb, (2, 0, 1))
        pb = jnp.tile(pb[None], (bsz, 1, 1, 1)).reshape(bsz * nh, tgt_len, src_len)
        query_layer = q.reshape(bsz, nh, tgt_len, hd) * ALPHA / scaling
        gate = jax.nn.sigmoid((query_layer @ grep_w + grep_b).sum(-1, keepdims=True))
        gate = (gate * grep_a).reshape(bsz * nh, tgt_len, 1)
        attn_weights = attn_weights + gate * pb
        probs = jax.nn.softmax(attn_weights, axis=-1)
        attn = jnp.einsum('bts,bsh->bth', probs, v)
        attn = attn.reshape(bsz, nh, tgt_len, hd)
        attn = jnp.transpose(attn, (2, 0, 1, 3)).reshape(tgt_len, bsz, embed_dim)
        return attn @ out_w + out_b

    def _L1_xattn_ref(q, k, v, Wq, Wk, Wv, Wo):
        import jax, jax.numpy as jnp
        import numpy as np
        DIM = 128
        N_HEADS = 16
        HEAD_DIM = DIM // N_HEADS
        B, L, M = (2, 256, 256)
        b, l, _ = q.shape
        m = k.shape[1]
        qp = q @ Wq.T
        kp = k @ Wk.T
        vp = v @ Wv.T
        qh = qp.reshape(b, l, HEAD_DIM, N_HEADS)
        kh = kp.reshape(b, m, HEAD_DIM, N_HEADS)
        score = jnp.einsum('bldn,bmdn->blmn', qh, kh) / jnp.sqrt(jnp.float32(HEAD_DIM))
        attn = jax.nn.softmax(score, axis=2)
        x = jnp.einsum('blmn,bmdn->bldn', attn, kh)
        x = x.reshape(b, l, DIM)
        return x @ Wo.T

    def _L1_ffn_ref(hidden_states, router_w, e_bias, Wg, Wu, Wd, SWg, SWu, SWd):
        import jax, jax.numpy as jnp
        import numpy as np
        H = 128
        I = 64
        E = 64
        G = 8
        TOPK_GROUP = 4
        K = 8
        I_SH = 128
        SCALE = 2.5

        def _route(x, router_w, e_bias):
            T = x.shape[0]
            scores = jax.nn.sigmoid(x.astype(jnp.float32) @ router_w.T.astype(jnp.float32))
            sfc = jax.lax.stop_gradient(scores) + e_bias[None, :]
            group_scores = jax.lax.top_k(sfc.reshape(T, G, E // G), 2)[0].sum(-1)
            _, gidx = jax.lax.top_k(group_scores, TOPK_GROUP)
            gmask = jax.nn.one_hot(gidx, G, dtype=sfc.dtype).sum(1)
            smask = jnp.repeat(gmask, E // G, axis=1)
            masked = jnp.where(smask > 0, sfc, 0.0)
            _, topk_idx = jax.lax.top_k(masked, K)
            w = jnp.take_along_axis(scores, topk_idx, axis=1)
            w = w / (w.sum(-1, keepdims=True) + 1e-20)
            return (topk_idx, w * SCALE)
        orig_shape = hidden_states.shape
        x = hidden_states.reshape(-1, orig_shape[-1])
        T = x.shape[0]
        topk_idx, topk_w = _route(x, router_w, e_bias)
        coef = jnp.zeros((T, E), topk_w.dtype).at[jnp.arange(T)[:, None], topk_idx].add(topk_w)
        g = jnp.einsum('th,ehi->tei', x, Wg)
        u = jnp.einsum('th,ehi->tei', x, Wu)
        h = jax.nn.silu(g) * u * coef[:, :, None]
        moe_out = jnp.einsum('tei,eih->th', h, Wd)
        shared = jax.nn.silu(x @ SWg) * (x @ SWu) @ SWd
        return (moe_out + shared).reshape(orig_shape)
    x = _layernorm(x + _L0_attn_ref(x, L0_attn_Wq, L0_attn_Wk, L0_attn_Wv, L0_attn_Wo, L0_attn_proj, L0_attn_W1, L0_attn_b1, L0_attn_W2, L0_attn_b2, L0_attn_ln1_g, L0_attn_ln1_b, L0_attn_ln2_g, L0_attn_ln2_b), axis=-1)
    x = _layernorm(x + _L0_xattn_ref(x, ctx_1024, L0_xattn_w_sim, L0_xattn_b_sim, L0_xattn_W_qv, L0_xattn_b_qv), axis=-1)
    x = _layernorm(x + _L0_ffn_ref(x, L0_ffn_packed_weight, L0_ffn_weight_scale, L0_ffn_bias), axis=-1)
    x = _layernorm(x + _L1_attn_ref(x, L1_attn_q_w, L1_attn_q_b, L1_attn_k_w, L1_attn_k_b, L1_attn_v_w, L1_attn_v_b, L1_attn_out_w, L1_attn_out_b, L1_attn_rel_emb, L1_attn_grep_w, L1_attn_grep_b, L1_attn_grep_a, L1_attn_bias_k, L1_attn_bias_v), axis=-1)
    x = _layernorm(x + _L1_xattn_ref(x, ctx_1024, ctx_1024, L1_xattn_Wq, L1_xattn_Wk, L1_xattn_Wv, L1_xattn_Wo), axis=-1)
    x = _layernorm(x + _L1_ffn_ref(x, L1_ffn_router_w, L1_ffn_e_bias, L1_ffn_Wg, L1_ffn_Wu, L1_ffn_Wd, L1_ffn_SWg, L1_ffn_SWu, L1_ffn_SWd), axis=-1)
    return x

_drawn_inputs = setup_inputs


def setup_inputs(seed=0):
    import zlib

    import numpy as np

    out = dict(_drawn_inputs(seed))
    spreads = {'L0_attn_b1': (0.0, 0.468),
     'L0_attn_b2': (0.0, 0.1),
     'L0_attn_ln1_g': (1.0, 0.2),
     'L0_attn_ln1_b': (0.0, 0.1),
     'L0_attn_ln2_g': (1.0, 0.2),
     'L0_attn_ln2_b': (0.0, 0.1),
     'L0_ffn_bias': (0.0, 0.1),
     'L1_attn_q_b': (0.0, 0.8),
     'L1_attn_k_b': (0.0, 0.8),
     'L1_attn_v_b': (0.0, 0.8),
     'L1_attn_out_b': (0.0, 0.1),
     'L1_attn_grep_b': (0.0, 0.8),
     'L1_attn_grep_a': (1.0, 0.6),
     'L1_ffn_e_bias': (0.0, 0.8)}
    factors = {'L0_attn_Wq': 64.0,
     'L0_attn_Wk': 64.0,
     'L0_attn_Wv': 6.456,
     'L0_attn_Wo': 6.55,
     'L0_attn_proj': 64.0,
     'L0_xattn_b_qv': 2.787,
     'L1_attn_q_w': 8.0,
     'L1_attn_k_w': 8.0,
     'L1_attn_v_w': 8.0,
     'L1_attn_out_w': 7.573,
     'L1_attn_rel_emb': 8.0,
     'L1_attn_grep_w': 8.0,
     'L1_attn_bias_k': 64.0,
     'L1_attn_bias_v': 42.347,
     'L1_ffn_router_w': 8.0,
     'L1_ffn_Wg': 8.0,
     'L1_ffn_Wu': 8.0,
     'L1_ffn_Wd': 8.0,
     'L1_ffn_SWg': 8.0,
     'L1_ffn_SWu': 8.0,
     'L1_ffn_SWd': 8.0}
    for name, (base, spread) in spreads.items():
        noise = np.random.default_rng([zlib.crc32(name.encode()), seed]).standard_normal(out[name].shape)
        drawn = base * np.exp(spread * noise) if base else spread * noise
        out[name] = jnp.asarray(drawn.astype(out[name].dtype))
    for name, factor in factors.items():
        out[name] = (out[name] * factor).astype(out[name].dtype)
    return out
```

```python
from contextlib import ExitStack

import concourse.bass as bass
import concourse.mybir as mybir
import numpy as np

F32 = mybir.dt.float32
F16 = mybir.dt.float16
I32 = mybir.dt.int32
ACT = mybir.ActivationFunctionType
ALU = mybir.AluOpType
AX = mybir.AxisListType.X

B, S, D = 128, 64, 128
TOK = B * S
P = 128
TILES = TOK // P
H = 16
EPS_OUT = 1e-5


class Phase:

    def __init__(self, nc, name):
        self.nc, self.name, self.ctx = nc, name, ExitStack()
        self.sems = []

    def __enter__(self):
        return self

    def __exit__(self, *exc):
        if self.sems:
            self.nc.clear_and_free_semaphores(self.sems)
            self.nc.all_engine_barrier()
        return self.ctx.__exit__(*exc)

    def sb(self, name, shape, dt=F32):
        return self.ctx.enter_context(self.nc.sbuf_tensor(f"{self.name}_{name}", shape, dt))

    def ps(self, name, shape, dt=F32):
        return self.ctx.enter_context(self.nc.psum_tensor(f"{self.name}_{name}", shape, dt))

    def sem(self, name):
        self.sems.append(self.nc.alloc_semaphore(name=f"{self.name}_{name}"))
        return self.sems[-1]


def is_first(it):
    return isinstance(it, int) and it == 0


def peeled(eng, steps, body):
    body(0)
    with eng.Fori(1, steps) as it:
        body(it)


class Own:

    def __init__(self, eng, sem):
        self.eng, self.sem = eng, sem
        self.done, self.at, self.per_step, self.base = 0, 0, None, 0

    def step(self, it):
        if not is_first(it) and self.per_step is None:
            self.per_step = self.at
        self.at = 0
        self.base = 0 if is_first(it) else self.per_step * it

    def mark(self, ins):
        ins.then_inc(self.sem, 1)
        self.at += 1
        return self.base + self.at

    def wait(self, mark):
        self.eng.wait_ge(self.sem, mark)


class Norms:

    def __init__(self, ph, U, per_step):
        self.U, self.per_step = U, per_step
        self.bn = [ph.sb(f"bn{j}", [P, 6]) for j in range(U)]
        self.mv = [ph.sb(f"mv{j}", [P, 2]) for j in range(U)]
        self.var_eps = [ph.sb(f"var_eps{j}", [P, 1]) for j in range(U)]
        self.rstd = [ph.sb(f"rstd{j}", [P, 1]) for j in range(U)]
        self.minus_half = ph.sb("minus_half", [P, 1])
        self.var_ready, self.rstd_ready, self.waited = ph.sem("var_ready"), ph.sem("rstd_ready"), ph.sem("bn_waited")
        self.power_const = ph.sem("power_const")

    def nth(self, it, k, j):
        return self.per_step * self.U * it + k * self.U + j + 1

    def stats(self, nc, own, src, eps, wait):
        dve = nc.vector
        marks = []
        for j in range(self.U):
            wait(j)
            marks.append(own.mark(dve.bn_stats(self.bn[j][:], src[j])))
        for j in range(self.U):
            own.wait(marks[j])
            dve.sem_inc(self.waited, 1)
            marks[j] = own.mark(dve.bn_aggr(self.mv[j][:], self.bn[j][:]))
        for j in range(self.U):
            own.wait(marks[j])
            dve.tensor_scalar(self.var_eps[j][:], self.mv[j][:, 1:2], eps, None, ALU.add).then_inc(self.var_ready, 1)

    def setup_power(self, nc):
        nc.gpsimd.memset(self.minus_half[:], -0.5).then_inc(self.power_const, 1)
        nc.gpsimd.wait_ge(self.power_const, 1)

    def power(self, nc, it, k):
        for j in range(self.U):
            nc.gpsimd.wait_ge(self.var_ready, self.nth(it, k, j))
            nc.gpsimd.tensor_tensor(self.rstd[j][:], self.var_eps[j][:], self.minus_half[:], ALU.pow).then_inc(self.rstd_ready, 1)

    def apply(self, nc, it, k, j, src, out):
        nc.vector.wait_ge(self.rstd_ready, self.nth(it, k, j))
        return nc.vector.tensor_scalar(out, src, self.mv[j][:, 0:1], self.rstd[j][:], ALU.subtract, ALU.mult)


def make_ident(nc, ph):
    ident = ph.sb("ident", [P, P])
    zeroed, ident_ready = ph.sem("zeroed"), ph.sem("ident_ready")
    with nc.Block() as block:
        @block.gpsimd
        def _(pool):
            nc.gpsimd.memset(ident[:], 0.0).then_inc(zeroed, 1)
            pool.wait_ge(zeroed, 1)
            nc.gpsimd.affine_select(out=ident[:], in_=ident[:], compare_op=ALU.not_equal, fill=1.0,
                                    base=0, pattern=[[-1, P]], channel_multiplier=1).then_inc(ident_ready, 1)
            pool.wait_ge(ident_ready, 1)
    return ident


L0_SCALE = dict(Wq=16.0, Wk=16.0, Wv=64.0, Wqp=1.0, Wkp=1.0)


def thrice(nc, out, lhsT, rhs, start=True, stop=True):
    nc.tensor.matmul(out, lhsT[0], rhs[0], start=start, stop=False)
    nc.tensor.matmul(out, lhsT[0], rhs[1], start=False, stop=False)
    return nc.tensor.matmul(out, lhsT[1], rhs[0], start=False, stop=stop)


def setup_l0(nc, ph, d, ident):
    DH, PAIRS = 64, H // 2
    DN = float(DH) ** -0.25
    PROJECTED = ("Wq", "Wk", "Wv", "Wqp", "Wkp")
    w = {k: [ph.sb(f"{k}_{part}", [P, PAIRS, P], F16) for part in ("high", "low")] for k in PROJECTED}
    w["Wo"] = ph.sb("Wo", [P, PAIRS, P])
    w.update(W1=ph.sb("W1", [D, 4 * P]), W2=ph.sb("W2", [P, 4, D]), b1_parts=ph.sb("b1_parts", [2, 4 * P], F16),
             b2_parts=ph.sb("b2_parts", [2, D], F16), ones2=ph.sb("ones2", [2, P], F16), ident=ident,
             key_max=ph.sb("key_max", [P, 1]), ln1_g=ph.sb("ln1_g", [P, D]), ln1_b=ph.sb("ln1_b", [P, D]),
             ln2_g=ph.sb("ln2_g", [P, D]), ln2_b=ph.sb("ln2_b", [P, D]))
    with Phase(nc, "s0") as t:
        wT = {k: t.sb(k, [P, PAIRS, D]) for k in ("WqT", "WkT")}
        whole = {k: t.sb(k, [P, PAIRS, P]) for k in PROJECTED}
        projT2 = t.sb("projT2", [P, DH])
        b1_rows, b2_rows, low_row = t.sb("b1_rows", [2, 4 * P]), t.sb("b2_rows", [2, D]), t.sb("low_row", [2, 1])
        fused = [t.ps(f"fused{i}", [P, PAIRS, DH]) for i in range(4)]
        loaded, ones_ready, joined, scaled, high_ready, masked = (
            t.sem(n) for n in ("loaded", "ones_ready", "joined", "scaled", "high_ready", "masked"))
        loads = [(whole["Wq"], d["Wq"]), (whole["Wk"], d["Wk"]), (whole["Wv"], d["Wv"]), (w["Wo"], d["Wo"]), (wT["WqT"], d["WqT"]),
                 (wT["WkT"], d["WkT"]), (w["W1"], d["W1"]), (w["W2"], d["W2"]), (b1_rows, d["b1"].to_broadcast([2, 4 * P])), (b2_rows, d["b2"].to_broadcast([2, D])), (low_row, d["low_row"]),
                 (w["ln1_g"], d["ln1_g"].to_broadcast([P, D])), (w["ln1_b"], d["ln1_b"].to_broadcast([P, D])),
                 (w["ln2_g"], d["ln2_g"].to_broadcast([P, D])), (w["ln2_b"], d["ln2_b"].to_broadcast([P, D]))]
        with nc.Block() as block:
            @block.sync
            def _(sp):
                for dst, src in loads:
                    sp.dma_start(dst[:], src[:]).then_inc(loaded, 16)
                for half in (slice(0, 64), slice(64, 128)):
                    sp.dma_start(projT2[half, :], d["projT"][:]).then_inc(loaded, 16)

            @block.gpsimd
            def _(pool):
                nc.gpsimd.memset(w["ones2"][:], 1.0).then_inc(ones_ready, 1)

            @block.tensor
            def _(pe):
                pe.wait_ge(loaded, 16 * (len(loads) + 2))
                for n, name in enumerate(("WqT", "WkT")):
                    for h in range(H):
                        half = slice(64 * (h % 2), 64 * (h % 2) + 64)
                        last = nc.tensor.matmul(fused[2 * n + h % 2][:, h // 2, :], wT[name][half, h // 2, :],
                                                projT2[half, :], start=True, stop=True)
                last.then_inc(joined, 1)

            @block.vector
            def _(dve):
                dve.wait_ge(joined, 1)
                for n, name in enumerate(("Wqp", "Wkp")):
                    for hh in range(2):
                        last = nc.vector.tensor_scalar(whole[name][:, :, 64 * hh:64 * hh + 64], fused[2 * n + hh][:], DN, None, ALU.mult)
                last.then_inc(scaled, 1)
                for n, k in enumerate(PROJECTED):
                    dve.wait_ge(high_ready, n + 1)
                    nc.vector.scalar_tensor_tensor(w[k][1][:].rearrange("p a b -> p (a b)"), whole[k][:].rearrange("p a b -> p (a b)"), L0_SCALE[k],
                                                   w[k][0][:].rearrange("p a b -> p (a b)"), ALU.mult, ALU.subtract)
                for n, (rows, parts) in enumerate(((b1_rows, w["b1_parts"]), (b2_rows, w["b2_parts"]))):
                    dve.wait_ge(high_ready, len(PROJECTED) + n + 1)
                    nc.vector.tensor_scalar(parts[:], parts[:], low_row[:], None, ALU.mult).then_inc(masked, 1)
                    dve.wait_ge(masked, n + 1)
                    nc.vector.tensor_tensor(parts[:], rows[:], parts[:], ALU.subtract)
                dve.wait_ge(ones_ready, 1)

            @block.scalar
            def _(act):
                act.wait_ge(loaded, 16 * (len(loads) + 2))
                for n, k in enumerate(PROJECTED):
                    if n == 3:
                        act.wait_ge(scaled, 1)
                    nc.scalar.activation(w[k][0][:], whole[k][:], ACT.Copy, scale=L0_SCALE[k]).then_inc(high_ready, 1)
                for rows, parts in ((b1_rows, w["b1_parts"]), (b2_rows, w["b2_parts"])):
                    nc.scalar.activation(parts[:], rows[:], ACT.Copy).then_inc(high_ready, 1)
    return w


def setup_cross0(nc, ph, d, ident):
    w = dict(ident=ident, Wqv=ph.sb("Wqv", [D, 4, D]), w1=ph.sb("w1", [D, 1]), w2=ph.sb("w2", [D, 1]), w3=ph.sb("w3", [D, 1]),
             b_sim=ph.sb("b_sim", [P, 1]), bqv_row=ph.sb("bqv_row", [1, D]), ternT=ph.sb("ternT", [D, 4, 32]),
             scale127=ph.sb("scale127", [P, 1]), ffn_bias=ph.sb("ffn_bias", [P, D]), ones_row=ph.sb("ones_row", [1, P]))
    with Phase(nc, "s2") as t:
        packed = t.sb("packed", [D, 32], I32)
        bits = t.sb("bits", [D, 4, 32], I32)
        loaded, unpacked = t.sem("loaded"), t.sem("unpacked")
        loads = [(w["Wqv"], d["Wqv"]), (w["w1"], d["w1"]), (w["w2"], d["w2"]), (w["w3"], d["w3"]),
                 (w["b_sim"], d["b_sim"].to_broadcast([P, 1])), (w["bqv_row"], d["b_qv"]), (packed, d["packed"]),
                 (w["scale127"], d["ternary_scale"].to_broadcast([P, 1])), (w["ffn_bias"], d["ffn_bias"].to_broadcast([P, D]))]
        with nc.Block() as block:
            @block.sync
            def _(sp):
                for dst, src in loads:
                    sp.dma_start(dst[:], src[:]).then_inc(loaded, 16)

            @block.vector
            def _(dve):
                nc.vector.memset(w["ones_row"][:], 1.0)
                dve.wait_ge(loaded, 16 * len(loads))
                for s in range(4):
                    nc.vector.tensor_scalar(bits[:, s, :], packed[:], 2 * s, 3, ALU.logical_shift_right, ALU.bitwise_and).then_inc(unpacked, 1)
                dve.wait_ge(unpacked, 4)
                nc.vector.tensor_scalar(w["ternT"][:], bits[:], -1.0, None, ALU.add)
                nc.vector.tensor_scalar(w["scale127"][:], w["scale127"][:], 1.0 / 127.0, None, ALU.mult).then_inc(unpacked, 1)
                dve.wait_ge(unpacked, 5)
    w["ternT"] = w["ternT"][:].rearrange("p a b -> p (a b)")
    return w


def phase_max(nc, xT, Wkp, shared_mx, xT_parts):
    GROUP, U, TILES_HM = 512, 2, 8
    steps = TOK // (GROUP * U)
    with Phase(nc, "mx") as ph:
        x_sb = [ph.sb(f"x{j}", [P, GROUP]) for j in range(U)]
        dd = [ph.ps(f"dd{i}", [P, 512]) for i in range(TILES_HM)]
        part = [ph.sb(f"part{j}", [P, TILES_HM]) for j in range(U)]
        acc = ph.sb("acc", [P, TILES_HM])
        col = ph.sb("col", [P, 1])
        one = ph.sb("one", [1, 1])
        ones_row = ph.sb("ones_row", [1, P])
        loaded = [ph.sem(f"loaded{j}") for j in range(U)]
        dd_ready, part_ready, acc_ready, small, moved, high_ready, low_ready = (
            ph.sem(n) for n in ("dd_ready", "part_ready", "acc_ready", "small", "moved", "high_ready", "low_ready"))
        ident = shared_mx["ident"]

        def group(it, j):
            return bass.ds((U * it + j) * GROUP, GROUP)

        with nc.Block() as block:
            @block.sync
            def _(sp):
                def body(it):
                    for j in range(U):
                        if not is_first(it):
                            sp.wait_ge(low_ready, U * it + (j + 1 - U))
                        sp.dma_start(x_sb[j][:], xT[:, bass.ds((U * it + j) * GROUP, GROUP)]).then_inc(loaded[j], 16)
                peeled(nc.sync, steps, body)

            @block.scalar
            def _(act):
                def body(it):
                    for j in range(U):
                        act.wait_ge(loaded[j], 16 * (it + 1))
                        nc.scalar.activation(xT_parts[0][:, group(it, j)], x_sb[j][:], ACT.Copy).then_inc(high_ready, 1)
                peeled(nc.scalar, steps, body)

            @block.gpsimd
            def _(pool):
                def body(it):
                    for j in range(U):
                        pool.wait_ge(high_ready, U * it + j + 1)
                        nc.gpsimd.tensor_tensor(xT_parts[1][:, group(it, j)], x_sb[j][:], xT_parts[0][:, group(it, j)], ALU.subtract).then_inc(low_ready, 1)
                peeled(nc.gpsimd, steps, body)

            @block.tensor
            def _(pe):
                def body(it):
                    for j in range(U):
                        pe.wait_ge(low_ready, U * it + j + 1)
                        for i in range(TILES_HM):
                            if not (is_first(it) and j == 0):
                                pe.wait_ge(part_ready, TILES_HM * (U * it + j - 1) + i + 1)
                            thrice(nc, dd[i][:], [part[:, i, :] for part in Wkp], [part[:, group(it, j)] for part in xT_parts]).then_inc(dd_ready, 1)
                peeled(nc.tensor, steps, body)
                pe.wait_ge(small, 1)
                nc.tensor.transpose(dd[0][0:1, 0:P], col[:], ident[:]).then_inc(moved, 1)
                pe.wait_ge(small, 2)
                nc.tensor.matmul(dd[1][:, 0:1], ones_row[:], one[:], start=True, stop=True).then_inc(moved, 1)

            @block.vector
            def _(dve):
                nc.vector.memset(acc[:], -3.0e38).then_inc(acc_ready, 1)
                nc.vector.memset(ones_row[:], 1.0)

                def body(it):
                    for j in range(U):
                        for i in range(TILES_HM):
                            n = TILES_HM * (U * it + j) + i + 1
                            dve.wait_ge(dd_ready, n)
                            nc.vector.tensor_reduce(part[j][:, i:i + 1], dd[i][:], AX, ALU.max).then_inc(part_ready, 1)
                        dve.wait_ge(part_ready, TILES_HM * (U * it + j + 1))
                        dve.wait_ge(acc_ready, U * it + j + 1)
                        nc.vector.tensor_tensor(acc[:], acc[:], part[j][:], ALU.max).then_inc(acc_ready, 1)
                peeled(nc.vector, steps, body)
                dve.wait_ge(acc_ready, U * steps + 1)
                nc.vector.tensor_reduce(col[:], acc[:], AX, ALU.max).then_inc(small, 1)
                dve.wait_ge(moved, 1)
                nc.vector.tensor_reduce(one[:], dd[0][0:1, 0:P], AX, ALU.max).then_inc(small, 1)
                dve.wait_ge(moved, 2)
                nc.vector.tensor_copy(shared_mx["key_max"][:], dd[1][:, 0:1]).then_inc(small, 1)
                dve.wait_ge(small, 3)


def phase_performer(nc, w, x, xT_parts, y1):
    U, DH, PAIRS = 2, 64, H // 2
    HALF = [slice(0, 64), slice(64, 128)]
    EPS_KERN = 1e-6
    DIAG = float(DH) ** -0.5 / 2.0
    steps = TILES // U
    Wq, Wk, Wv, Wqp, Wkp, Wo = (w[k] for k in ("Wq", "Wk", "Wv", "Wqp", "Wkp", "Wo"))

    with Phase(nc, "b1") as ph:
        x_sb = [ph.sb(f"x{j}", [P, D]) for j in range(U)]
        sq = [ph.sb(f"sq{j}", [P, H, DH]) for j in range(U)]
        e_sb = [ph.sb(f"e{j}", [P, H, DH]) for j in range(U)]
        qfT = [ph.sb(f"qfT{j}", [P, PAIRS, P]) for j in range(U)]
        kf = [ph.sb(f"kf{j}", [P, H, DH]) for j in range(U)]
        v_sb = [ph.sb(f"v{j}", [P, H, DH + 1]) for j in range(U)]
        kv = [[ph.sb(f"kv{j}{b}", [P, PAIRS, 2, DH + 1]) for b in range(2)] for j in range(U)]
        rden = [ph.sb(f"rden{j}", [P, H]) for j in range(U)]
        attn = [ph.sb(f"attn{j}", [P, PAIRS, P]) for j in range(U)]
        attnT = [ph.sb(f"attnT{j}", [P, PAIRS, P]) for j in range(U)]
        stat = [ph.sb(f"stat{j}", [P, 3, H]) for j in range(U)]
        qn = [stat[j][:, 0, :] for j in range(U)]
        shift = [stat[j][:, 1, :] for j in range(U)]
        top = [stat[j][:, 2, :] for j in range(U)]
        y = [ph.sb(f"y{j}", [P, D]) for j in range(U)]
        eps_kern = ph.sb("eps_kern", [P, 1])
        ps_a = [ph.ps(f"a{j}", [P, 2, 512]) for j in range(U)]
        ps_b = [ph.ps(f"b{j}", [P, 2, 512]) for j in range(U)]

        loaded = [ph.sem(f"loaded{j}") for j in range(U)]
        stored = [ph.sem(f"stored{j}") for j in range(U)]
        (consts, q_ready, q_squared, qn_ready, dq_ready, dq_shifted, q_exp, qfT_ready, qfT_copied, k_ready,
         k_squared, dk_ready, dk_shifted, k_exp, kf_ready, v_ready, v_copied, kv_ready, kv0_copied, kv1_copied,
         num_ready, attn_ready, proj_ready, y_ready, dve_own) = (
            ph.sem(n) for n in (
                "consts", "q_ready", "q_squared", "qn_ready", "dq_ready", "dq_shifted", "q_exp", "qfT_ready",
                "qfT_copied", "k_ready", "k_squared", "dk_ready", "dk_shifted", "k_exp", "kf_ready", "v_ready",
                "v_copied", "kv_ready", "kv0_copied", "kv1_copied", "num_ready", "attn_ready", "proj_ready",
                "y_ready", "dve_own"))
        attn_done, turned = ph.sem("attn_done"), ph.sem("turned")
        waited = ph.sem("waited")

        def flat(t):
            return t[:].rearrange("p a b -> p (a b)")

        def heads(t):
            return flat(t).rearrange("p (h m) -> p h m", h=H)

        def pairs(t):
            return flat(t).rearrange("p (q n) -> p q n", q=PAIRS)

        def kv_banks(t):
            return t[:, :, 0:4 * (DH + 1)].rearrange("p g (q e) -> p g q e", e=DH + 1)

        def nth(it, j):
            return U * it + j + 1

        def before(it, j):
            return U * it + (j + 1 - U)

        def blocks_copy(copy, j, b):
            src = kv_banks((ps_a, ps_b)[b][j])
            for hh in range(2):
                last = copy(kv[j][b][HALF[hh], :, hh, :].rearrange("p (g q) e -> p g q e", g=2), src[HALF[hh]])
            return last

        def weighed(j):
            def pairs_in(bank, n):
                return bank[:, 0:n * 2 * (DH + 1)].rearrange("p (q a e) -> p q a e", a=2, e=DH + 1)

            return [(pairs_in(ps_a[j][:, 0, :], 3), slice(0, 3)), (pairs_in(ps_a[j][:, 1, :], 3), slice(3, 6)), (pairs_in(ps_b[j][:, 0, :], 2), slice(6, 8))]

        with nc.Block() as block:
            @block.sync
            def _(sp):
                def body(it):
                    for j in range(U):
                        if not is_first(it):
                            sp.wait_ge(y_ready, before(it, j))
                            sp.dma_start(y1[bass.ds((U * it + (j - U)) * P, P), :], y[j][:]).then_inc(stored[j], 16)
                        sp.dma_start(x_sb[j][:], x[bass.ds((U * it + j) * P, P), :]).then_inc(loaded[j], 16)
                peeled(nc.sync, steps, body)
                for j in range(U):
                    sp.wait_ge(y_ready, nth(steps - 1, j))
                    sp.dma_start(y1[(TILES - U + j) * P:(TILES - U + j + 1) * P, :], y[j][:]).then_inc(stored[j], 16)
                for j in range(U):
                    sp.wait_ge(stored[j], 16 * steps)

            @block.gpsimd
            def _(pool):
                for j in range(U):
                    for b in range(2):
                        nc.gpsimd.memset(kv[j][b][:], 0.0)
                    nc.gpsimd.memset(v_sb[j][:], 1.0)
                nc.gpsimd.memset(eps_kern[:], EPS_KERN).then_inc(consts, 1)

            @block.tensor
            def _(pe):
                pe.wait_ge(consts, 1)

                def wide(it, out, j, weights):
                    tile = bass.ds((U * it + j) * P, P)
                    for g in range(2):
                        last = thrice(nc, out[:, g, :], [part[:, tile] for part in xT_parts],
                                      [part[:, 4 * g:4 * g + 4, :].rearrange("p a b -> p (a b)") for part in weights])
                    return last

                def body(it):
                    for j in range(U):
                        if not is_first(it):
                            pe.wait_ge(y_ready, before(it, j))
                        wide(it, ps_a[j], j, Wq).then_inc(q_ready, 1)
                        wide(it, ps_b[j], j, Wqp).then_inc(dq_ready, 1)
                    for j in range(U):
                        pe.wait_ge(dq_shifted, nth(it, j))
                        wide(it, ps_b[j], j, Wk).then_inc(k_ready, 1)
                    for j in range(U):
                        pe.wait_ge(q_squared, nth(it, j))
                        pe.wait_ge(q_exp, nth(it, j))
                        for q in range(PAIRS):
                            last = nc.tensor.transpose(pairs(ps_a[j])[:, q, :],
                                                       e_sb[j][:, 2 * q:2 * q + 2, :].rearrange("p h m -> p (h m)"),
                                                       w["ident"][:])
                        last.then_inc(qfT_ready, 1)
                    for j in range(U):
                        pe.wait_ge(qfT_copied, nth(it, j))
                        wide(it, ps_a[j], j, Wkp).then_inc(dk_ready, 1)
                    for j in range(U):
                        pe.wait_ge(k_squared, nth(it, j))
                        wide(it, ps_b[j], j, Wv).then_inc(v_ready, 1)
                    for j in range(U):
                        pe.wait_ge(kf_ready, nth(it, j))
                        pe.wait_ge(v_copied, nth(it, j))
                        pe.sem_inc(waited, 1)
                        for b, out in ((0, ps_a[j]), (1, ps_b[j])):
                            for h in range(H):
                                q, hh = h // 2, h % 2
                                last = nc.tensor.matmul(kv_banks(out)[HALF[hh], q // 4, q % 4, :],
                                                        kf[j][HALF[b], h, :], v_sb[j][HALF[b], h, :],
                                                        start=True, stop=True)
                        last.then_inc(kv_ready, 1)
                    for j in range(U):
                        pe.wait_ge(kv0_copied, nth(it, j))
                        pe.wait_ge(kv1_copied, nth(it, j))
                        for b in range(2):
                            for out, qs in weighed(j):
                                for q in range(qs.start, qs.stop):
                                    last = nc.tensor.matmul(out[HALF[b], q - qs.start].rearrange("p a e -> p (a e)"), qfT[j][:, q, HALF[b]],
                                                            kv[j][b][:, q].rearrange("p a e -> p (a e)"), start=True, stop=True)
                        last.then_inc(num_ready, 1)
                    for j in range(U):
                        pe.wait_ge(attn_done, nth(it, j))
                        for q in range(PAIRS):
                            last = nc.tensor.transpose(pairs(ps_a[j])[:, q, :], attn[j][:, q, :], w["ident"][:])
                        last.then_inc(turned, 1)
                    for j in range(U):
                        pe.wait_ge(attn_ready, nth(it, j))
                        for q in range(PAIRS):
                            last = nc.tensor.matmul(ps_b[j][:, 0, 0:D], attnT[j][:, q, :], Wo[:, q, :],
                                                    start=(q == 0), stop=(q == PAIRS - 1))
                        last.then_inc(proj_ready, 1)
                peeled(nc.tensor, steps, body)

            @block.scalar
            def _(act):
                act.wait_ge(consts, 1)
                def body(it):
                    for j in range(U):
                        act.wait_ge(q_ready, nth(it, j))
                        if not is_first(it):
                            act.wait_ge(dk_shifted, before(it, j))
                        nc.scalar.activation(sq[j][:], heads(ps_a[j]), ACT.Square, scale=1.0 / L0_SCALE["Wq"]).then_inc(q_squared, 1)
                    for j in range(U):
                        act.wait_ge(dq_shifted, nth(it, j))
                        nc.scalar.activation(e_sb[j][:], e_sb[j][:], ACT.Exp).then_inc(q_exp, 1)
                    for j in range(U):
                        act.wait_ge(k_ready, nth(it, j))
                        act.wait_ge(qn_ready, nth(it, j))
                        nc.scalar.activation(sq[j][:], heads(ps_b[j]), ACT.Square, scale=1.0 / L0_SCALE["Wk"]).then_inc(k_squared, 1)
                    for j in range(U):
                        act.wait_ge(qfT_ready, nth(it, j))
                        nc.scalar.activation(qfT[j][:], pairs(ps_a[j]), ACT.Identity, bias=eps_kern[:]).then_inc(qfT_copied, 1)
                    for j in range(U):
                        act.wait_ge(dk_shifted, nth(it, j))
                        nc.scalar.activation(kf[j][:], kf[j][:], ACT.Exp).then_inc(k_exp, 1)
                        act.wait_ge(v_ready, nth(it, j))
                        nc.scalar.activation(v_sb[j][:, :, 0:DH], heads(ps_b[j]), ACT.Copy).then_inc(v_copied, 1)
                    for j in range(U):
                        act.wait_ge(kv_ready, nth(it, j))
                        last = blocks_copy(lambda o, i: nc.scalar.activation(o, i, ACT.Copy), j, 1)
                        last.then_inc(kv1_copied, 1)
                    for j in range(U):
                        act.wait_ge(turned, nth(it, j))
                        nc.scalar.activation(attnT[j][:], pairs(ps_a[j]), ACT.Copy, scale=1.0 / L0_SCALE["Wv"]).then_inc(attn_ready, 1)
                peeled(nc.scalar, steps, body)

            @block.vector
            def _(dve):
                dve.wait_ge(consts, 1)
                own = Own(dve, dve_own)

                def body(it):
                    own.step(it)
                    for j in range(U):
                        dve.wait_ge(q_squared, nth(it, j))
                        nc.vector.tensor_reduce(qn[j], sq[j][:], AX, ALU.add).then_inc(qn_ready, 1)
                        dve.wait_ge(dq_ready, nth(it, j))
                        m = own.mark(nc.vector.tensor_reduce(top[j], heads(ps_b[j]), AX, ALU.max))
                        dve.wait_ge(qn_ready, nth(it, j))
                        own.wait(m)
                        m = own.mark(nc.vector.scalar_tensor_tensor(shift[j], qn[j], DIAG, top[j], ALU.mult, ALU.add))
                        own.wait(m)
                        nc.vector.tensor_tensor(e_sb[j][:], heads(ps_b[j]), shift[j].unsqueeze(2).to_broadcast([P, H, DH]),
                                                ALU.subtract).then_inc(dq_shifted, 1)
                    for j in range(U):
                        dve.wait_ge(k_squared, nth(it, j))
                        m = own.mark(nc.vector.tensor_reduce(qn[j], sq[j][:], AX, ALU.add))
                        own.wait(m)
                        m = own.mark(nc.vector.tensor_scalar(shift[j], qn[j], DIAG, w["key_max"][:], ALU.mult, ALU.add))
                        dve.wait_ge(dk_ready, nth(it, j))
                        own.wait(m)
                        nc.vector.tensor_tensor(kf[j][:], heads(ps_a[j]), shift[j].unsqueeze(2).to_broadcast([P, H, DH]),
                                                ALU.subtract).then_inc(dk_shifted, 1)
                    for j in range(U):
                        dve.wait_ge(k_exp, nth(it, j))
                        nc.vector.tensor_scalar(kf[j][:], kf[j][:], EPS_KERN, None, ALU.add).then_inc(kf_ready, 1)
                    for j in range(U):
                        dve.wait_ge(kv_ready, nth(it, j))
                        blocks_copy(nc.vector.tensor_copy, j, 0).then_inc(kv0_copied, 1)
                    for j in range(U):
                        dve.wait_ge(num_ready, nth(it, j))
                        for out, qs in weighed(j):
                            m = own.mark(nc.vector.reciprocal(rden[j][:, 2 * qs.start:2 * qs.stop].rearrange("p (q a) -> p q a", a=2), out[:, :, :, DH]))
                        own.wait(m)
                        for out, qs in weighed(j):
                            n = qs.stop - qs.start
                            last = nc.vector.tensor_tensor(attn[j][:, qs, :].rearrange("p q (a e) -> p q a e", a=2), out[:, :, :, 0:DH],
                                                           rden[j][:, 2 * qs.start:2 * qs.stop].rearrange("p (q a) -> p q a", a=2)
                                                           .unsqueeze(3).to_broadcast([P, n, 2, DH]), ALU.mult)
                        last.then_inc(attn_done, 1)
                    for j in range(U):
                        dve.wait_ge(proj_ready, nth(it, j))
                        dve.wait_ge(loaded[j], 16 * (it + 1))
                        if not is_first(it):
                            dve.wait_ge(stored[j], 16 * it)
                        nc.vector.tensor_tensor(y[j][:], ps_b[j][:, 0, 0:D], x_sb[j][:], ALU.add).then_inc(y_ready, 1)

                peeled(nc.vector, steps, body)



def phase_feed_forward0(nc, w, x, y1, x1):
    GROUP, FC, EPS_LN = 4, 4, 1e-6
    U = 2 * GROUP
    steps = TILES // U

    with Phase(nc, "f1") as ph:
        def slots(name, shape):
            return [ph.sb(f"{name}{j}", shape) for j in range(U)]

        x_sb, y, z, x_shifted, out1, out1T, res = (slots(n, [P, D]) for n in ("x", "y", "z", "x_shifted", "out1", "out1T", "res"))
        negative, positive = slots("negative", [P, FC * P]), slots("positive", [P, FC * P])
        bn, mv = slots("bn", [P, 6]), slots("mv", [P, 2])
        var_eps, rstd, minus_half = slots("var_eps", [P, 1]), slots("rstd", [P, 1]), ph.sb("minus_half", [P, 1])
        hidden = [ph.ps(f"hidden{i}", [P, FC * P]) for i in range(GROUP)]
        narrow = [ph.ps(f"narrow{i}", [P, 2, P]) for i in range(GROUP)]
        y_loaded = [ph.sem(f"y_loaded{j}") for j in range(U)]
        x_loaded = [ph.sem(f"x_loaded{j}") for j in range(U)]
        stored = [ph.sem(f"stored{j}") for j in range(U)]
        var_ready, rstd_ready, normed = ([ph.sem(f"{n}{k}") for k in range(3)] for n in ("var_ready", "rstd_ready", "normed"))
        names = ("consts", "scaled", "out1_ready", "out1T_ready", "out1T_copied", "hidden_ready", "min_ready", "exp_ready", "relu_ready",
                 "elu_ready", "ffn_ready", "ffn_added", "scaled2", "shifted2", "sum_ready", "own_first", "own_last", "waited")
        (consts, scaled, out1_ready, out1T_ready, out1T_copied, hidden_ready, min_ready, exp_ready, relu_ready,
         elu_ready, ffn_ready, ffn_added, scaled2, shifted2, sum_ready, own_first, own_last, waited) = (ph.sem(n) for n in names)

        def members(g):
            return [(i, GROUP * (g % 2) + i) for i in range(GROUP)]

        def nth(it, g, i):
            return U * it + GROUP * g + i + 1

        def rounds(it, g):
            return it + g // 2 + 1

        def is_start(it, g):
            return isinstance(it, int) and 2 * it + g == 0

        def turn_of(it, g):
            return g if is_first(it) else 2 * it + g

        def pipelined(eng, first, turn, last):
            def step(it, begins=False, ends=False):
                for g in range(2):
                    turn(it, g, None if begins and g == 0 else (it, g - 1), None if ends and g == 1 else (it, g + 1))
            for part in first:
                part(0, 0)
            step(0, begins=True)
            with eng.Fori(1, steps - 1) as it:
                step(it)
            step(steps - 1, ends=True)
            for part in last:
                part(steps - 1, 1)

        def run(part, group):
            if group is not None:
                part(*group)

        with nc.Block() as block:
            @block.sync
            def _(sp):
                def body(it):
                    for j in range(U):
                        tile = bass.ds((U * it + j) * P, P)
                        if not is_first(it):
                            sp.wait_ge(normed[0], U * it + j + 1 - U)
                        sp.dma_start(y[j][:], y1[tile, :]).then_inc(y_loaded[j], 16)
                        if not is_first(it):
                            sp.wait_ge(shifted2, U * it + j + 1 - U)
                        sp.dma_start(x_sb[j][:], x[tile, :]).then_inc(x_loaded[j], 16)
                    if not is_first(it):
                        for j in range(U):
                            sp.wait_ge(normed[2], U * it + j + 1 - U)
                            sp.dma_start(x1[bass.ds((U * it + (j - U)) * P, P), :], res[j][:]).then_inc(stored[j], 16)
                peeled(nc.sync, steps, body)
                for j in range(U):
                    sp.wait_ge(normed[2], U * (steps - 1) + j + 1)
                    sp.dma_start(x1[(TILES - U + j) * P:(TILES - U + j + 1) * P, :], res[j][:]).then_inc(stored[j], 16)
                for j in range(U):
                    sp.wait_ge(stored[j], 16 * steps)

            @block.gpsimd
            def _(pool):
                nc.gpsimd.memset(minus_half[:], -0.5).then_inc(consts, 1)
                pool.wait_ge(consts, 1)

                def power(it, g, k):
                    for i, s in members(g):
                        pool.wait_ge(var_ready[k], nth(it, g, i))
                        nc.gpsimd.tensor_tensor(rstd[s][:], var_eps[s][:], minus_half[:], ALU.pow).then_inc(rstd_ready[k], 1)

                def first_norm(it, g):
                    power(it, g, 0)
                    for i, s in members(g):
                        pool.wait_ge(normed[0], nth(it, g, i))
                        nc.gpsimd.tensor_tensor(z[s][:], z[s][:], w["ln1_g"][:], ALU.mult).then_inc(scaled, 1)
                    for i, s in members(g):
                        pool.wait_ge(scaled, nth(it, g, i))
                        nc.gpsimd.tensor_tensor(out1[s][:], z[s][:], w["ln1_b"][:], ALU.add).then_inc(out1_ready, 1)

                def last_norms(it, g):
                    for i, s in members(g):
                        pool.wait_ge(x_loaded[s], 16 * rounds(it, g))
                        nc.gpsimd.tensor_tensor(x_shifted[s][:], x_sb[s][:], w["ln2_b"][:], ALU.add).then_inc(shifted2, 1)
                    power(it, g, 1)
                    for i, s in members(g):
                        pool.wait_ge(normed[1], nth(it, g, i))
                        nc.gpsimd.tensor_tensor(z[s][:], z[s][:], w["ln2_g"][:], ALU.mult).then_inc(scaled2, 1)
                    for i, s in members(g):
                        pool.wait_ge(scaled2, nth(it, g, i))
                        pool.wait_ge(shifted2, nth(it, g, i))
                        nc.gpsimd.tensor_tensor(z[s][:], z[s][:], x_shifted[s][:], ALU.add).then_inc(sum_ready, 1)
                    power(it, g, 2)

                def turn(it, g, previous, following):
                    run(last_norms, previous)
                    run(first_norm, following)
                pipelined(nc.gpsimd, (first_norm,), turn, (last_norms,))

            @block.tensor
            def _(pe):
                def turn_tokens(it, g):
                    for i, s in members(g):
                        pe.wait_ge(out1_ready, nth(it, g, i))
                        if not is_start(it, g):
                            pe.wait_ge(ffn_added, nth(it, g, i) - GROUP)
                        nc.tensor.transpose(narrow[i][:, 0, :], out1[s][:], w["ident"][:]).then_inc(out1T_ready, 1)

                def up(it, g):
                    for i, s in members(g):
                        pe.wait_ge(out1T_copied, nth(it, g, i))
                        for c in range(FC):
                            cs = slice(c * P, (c + 1) * P)
                            nc.tensor.matmul(hidden[i][:, cs], w["b1_parts"][:, cs], w["ones2"][:], start=True, stop=False)
                            last = nc.tensor.matmul(hidden[i][:, cs], w["W1"][:, cs], out1T[s][:], start=False, stop=True)
                        last.then_inc(hidden_ready, 1)

                def down(it, g):
                    for i, s in members(g):
                        pe.wait_ge(elu_ready, nth(it, g, i))
                        nc.tensor.matmul(narrow[i][:, 1, :], w["ones2"][:], w["b2_parts"][:], start=True, stop=False)
                        for c in range(FC):
                            last = nc.tensor.matmul(narrow[i][:, 1, :], negative[s][:, c * P:(c + 1) * P], w["W2"][:, c, :],
                                                    start=False, stop=(c == FC - 1))
                        last.then_inc(ffn_ready, 1)

                def turn(it, g, previous, following):
                    turn_tokens(it, g)
                    up(it, g)
                    down(it, g)
                pipelined(nc.tensor, (), turn, ())

            @block.scalar
            def _(act):
                def turn(it, g, previous, following):
                    for i, s in members(g):
                        act.wait_ge(out1T_ready, nth(it, g, i))
                        nc.scalar.activation(out1T[s][:], narrow[i][:, 0, :], ACT.Copy).then_inc(out1T_copied, 1)
                    for i, s in members(g):
                        act.wait_ge(min_ready, nth(it, g, i))
                        nc.scalar.activation(positive[s][:], hidden[i][:], ACT.Relu).then_inc(relu_ready, 1)
                        nc.scalar.activation(negative[s][:], negative[s][:], ACT.Exp).then_inc(exp_ready, 1)
                pipelined(nc.scalar, (), turn, ())

            @block.vector
            def _(dve):
                first_own, last_own = Own(dve, own_first), Own(dve, own_last)

                def stats(own, it, g, k, src, wait, eps):
                    marks = []
                    for i, s in members(g):
                        wait(i, s)
                        marks.append(own.mark(nc.vector.bn_stats(bn[s][:], src[s][:])))
                    for i, s in members(g):
                        own.wait(marks[i])
                        dve.sem_inc(waited, 1)
                        marks[i] = own.mark(nc.vector.bn_aggr(mv[s][:], bn[s][:]))
                    for i, s in members(g):
                        own.wait(marks[i])
                        nc.vector.tensor_scalar(var_eps[s][:], mv[s][:, 1:2], eps, None, ALU.add).then_inc(var_ready[k], 1)

                def norm(it, g, k, src, out):
                    for i, s in members(g):
                        dve.wait_ge(rstd_ready[k], nth(it, g, i))
                        nc.vector.tensor_scalar(out[s][:], src[s][:], mv[s][:, 0:1], rstd[s][:], ALU.subtract, ALU.mult).then_inc(normed[k], 1)

                def first_norm(it, g):
                    first_own.step(turn_of(it, g))
                    stats(first_own, it, g, 0, y, lambda i, s: dve.wait_ge(y_loaded[s], 16 * rounds(it, g)), EPS_LN)
                    norm(it, g, 0, y, z)

                def second_norm(it, g):
                    last_own.step(turn_of(it, g))
                    stats(last_own, it, g, 1, z, lambda i, s: dve.wait_ge(ffn_added, nth(it, g, i)), EPS_LN)
                    norm(it, g, 1, z, z)

                def third_norm(it, g):
                    stats(last_own, it, g, 2, z, lambda i, s: dve.wait_ge(sum_ready, nth(it, g, i)), EPS_OUT)
                    for i, s in members(g):
                        if not (isinstance(it, int) and rounds(it, g) == 1):
                            dve.wait_ge(stored[s], 16 * (rounds(it, g) - 1))
                    norm(it, g, 2, z, res)

                def turn(it, g, previous, following):
                    run(second_norm, previous)
                    for i, s in members(g):
                        dve.wait_ge(hidden_ready, nth(it, g, i))
                        nc.vector.tensor_scalar(negative[s][:], hidden[i][:], 0.0, None, ALU.min).then_inc(min_ready, 1)
                    for i, s in members(g):
                        dve.wait_ge(relu_ready, nth(it, g, i))
                        dve.wait_ge(exp_ready, nth(it, g, i))
                        nc.vector.scalar_tensor_tensor(negative[s][:], negative[s][:], -1.0, positive[s][:], ALU.add, ALU.add).then_inc(elu_ready, 1)
                    run(third_norm, previous)
                    run(first_norm, following)
                    for i, s in members(g):
                        dve.wait_ge(ffn_ready, nth(it, g, i))
                        nc.vector.tensor_tensor(z[s][:], narrow[i][:, 1, :], out1[s][:], ALU.add).then_inc(ffn_added, 1)
                pipelined(nc.vector, (first_norm,), turn, (second_norm, third_norm))


def phase_cross0(nc, w, x1, ctx, ctxT, x3):
    U = 4
    HALF = [slice(0, S), slice(S, 2 * S)]
    ROUND = 12582912.0
    steps = TILES // U

    with Phase(nc, "b2") as ph:
        def slots(name, shape):
            return [ph.sb(f"{name}{j}", shape) for j in range(U)]

        x_sb, c_sb, cT_sb = slots("x", [P, D]), slots("c", [P, D]), slots("cT", [D, P])
        xT, lhs, E, ET = slots("xT", [D, P]), slots("lhs", [D, P]), slots("E", [P, P]), slots("ET", [P, P])
        hqT, x_hqT, x_hcT = slots("hqT", [D, P]), slots("x_hqT", [D, P]), slots("x_hcT", [D, P])
        negmax, total, peak = slots("negmax", [P, 1]), slots("total", [P, 1]), slots("peak", [P, 1])
        row, rowmax, bcol = slots("row", [1, 2, S]), slots("rowmax", [1, 2]), slots("bcol", [P, 1])
        y, x2, q8, q8T, res = slots("y", [P, D]), slots("x2", [P, D]), slots("q8", [P, D]), slots("q8T", [D, P]), slots("res", [P, D])
        magn, amax, step8 = slots("magn", [P, D]), slots("amax", [P, 1]), slots("step8", [P, 1])
        pa = [ph.ps(f"a{j}", [P, 512]) for j in range(U)]
        pb = [ph.ps(f"b{j}", [P, 512]) for j in range(U)]
        norms = Norms(ph, U, 2)
        loaded = [ph.sem(f"loaded{j}") for j in range(U)]
        stored = [ph.sem(f"stored{j}") for j in range(U)]
        (consts, xT_ready, xT_copied, lhs_ready, sim_ready, exp_ready, peak_ready, E_ready, ET_ready,
         ET_copied, row_ready, row_exp, row_done, hq_ready, bcol_copied, hqT_copied, hc_ready, feats_ready, mixed, x_added,
         x2_ready, magn_ready, q8_ready, q8T_ready, q8T_copied, ffn_ready, x3_ready, dve_own) = (ph.sem(n) for n in (
            "consts", "xT_ready", "xT_copied", "lhs_ready", "sim_ready", "exp_ready", "peak_ready",
            "E_ready", "ET_ready", "ET_copied", "row_ready", "row_exp", "row_done", "hq_ready", "bcol_copied",
            "hqT_copied", "hc_ready", "feats_ready", "mixed", "x_added", "x2_ready", "magn_ready", "q8_ready", "q8T_ready",
            "q8T_copied", "ffn_ready", "x3_ready", "dve_own"))

        def nth(it, j):
            return U * it + j + 1

        def before(it, j):
            return U * it + (j + 1 - U)

        with nc.Block() as block:
            @block.sync
            def _(sp):
                def body(it):
                    for j in range(U):
                        tile = bass.ds((U * it + j) * P, P)
                        if not is_first(it):
                            sp.wait_ge(x_added, before(it, j))
                        sp.dma_start(x_sb[j][:], x1[tile, :]).then_inc(loaded[j], 16)
                        sp.dma_start(c_sb[j][:], ctx[tile, :]).then_inc(loaded[j], 16)
                        sp.dma_start(cT_sb[j][:], ctxT[:, tile]).then_inc(loaded[j], 16)
                    if not is_first(it):
                        for j in range(U):
                            sp.wait_ge(x3_ready, before(it, j))
                            sp.dma_start(x3[bass.ds((U * it + (j - U)) * P, P), :], res[j][:]).then_inc(stored[j], 16)
                peeled(nc.sync, steps, body)
                for j in range(U):
                    sp.wait_ge(x3_ready, nth(steps - 1, j))
                    sp.dma_start(x3[(TILES - U + j) * P:(TILES - U + j + 1) * P, :], res[j][:]).then_inc(stored[j], 16)
                for j in range(U):
                    sp.wait_ge(stored[j], 16 * steps)

            @block.gpsimd
            def _(pool):
                for j in range(U):
                    last = nc.gpsimd.memset(E[j][:], 0.0)
                last.then_inc(consts, 1)
                norms.setup_power(nc)

                def body(it):
                    for k in range(2):
                        norms.power(nc, it, k)
                peeled(nc.gpsimd, steps, body)

            @block.tensor
            def _(pe):
                def body(it):
                    for j in range(U):
                        pe.wait_ge(loaded[j], 48 * (it + 1))
                        if not is_first(it):
                            pe.wait_ge(ffn_ready, before(it, j))
                            pe.wait_ge(x3_ready, before(it, j))
                        nc.tensor.transpose(pa[j][:, 0:P], x_sb[j][:], w["ident"][:]).then_inc(xT_ready, 1)
                    for j in range(U):
                        pe.wait_ge(xT_copied, nth(it, j))
                        pe.wait_ge(lhs_ready, nth(it, j))
                        nc.tensor.matmul(pb[j][:, S:S + 1], xT[j][:], w["w1"][:], start=True, stop=True)
                        for half in HALF:
                            last = nc.tensor.matmul(pb[j][half, 0:S], lhs[j][:, half], cT_sb[j][:, half], start=True, stop=True)
                        last.then_inc(sim_ready, 1)
                    for j in range(U):
                        pe.wait_ge(peak_ready, nth(it, j))
                        nc.tensor.transpose(pa[j][0:1, 256:384], peak[j][:], w["ident"][:])
                        pe.wait_ge(E_ready, nth(it, j))
                        nc.tensor.transpose(pa[j][:, 128:256], E[j][:], w["ident"][:]).then_inc(ET_ready, 1)
                    for j in range(U):
                        pe.wait_ge(ET_copied, nth(it, j))
                        pe.wait_ge(row_ready, nth(it, j))
                        nc.tensor.matmul(pa[j][:, 0:P], c_sb[j][:], ET[j][:], start=True, stop=True)
                        pe.wait_ge(row_done, nth(it, j))
                        nc.tensor.matmul(pb[j][:, 65:66], row[j][:].rearrange("o b i -> o (b i)"), w["ones_row"][0:1, 0:1],
                                         start=True, stop=True).then_inc(hq_ready, 1)
                    for j in range(U):
                        pe.wait_ge(hqT_copied, nth(it, j))
                        pe.wait_ge(bcol_copied, nth(it, j))
                        for b, out in ((0, pa[j]), (1, pb[j])):
                            last = nc.tensor.matmul(out[:, 400:401], x_sb[j][HALF[b], :], bcol[j][HALF[b], :], start=True, stop=True)
                        last.then_inc(hc_ready, 1)
                    for j in range(U):
                        pe.wait_ge(feats_ready, nth(it, j))
                        out = pb[j][:, 128:256]
                        nc.tensor.matmul(out, w["ones_row"][:], w["bqv_row"][:], start=True, stop=False)
                        for c, f in enumerate((xT, hqT, x_hqT, x_hcT)):
                            last = nc.tensor.matmul(out, f[j][:], w["Wqv"][:, c, :], start=False, stop=(c == 3))
                        last.then_inc(mixed, 1)
                    for j in range(U):
                        pe.wait_ge(q8_ready, nth(it, j))
                        nc.tensor.transpose(pa[j][:, 0:P], q8[j][:], w["ident"][:]).then_inc(q8T_ready, 1)
                    for j in range(U):
                        pe.wait_ge(q8T_copied, nth(it, j))
                        nc.tensor.matmul(pb[j][:, 0:D], q8T[j][:], w["ternT"][:], start=True, stop=True).then_inc(ffn_ready, 1)
                peeled(nc.tensor, steps, body)

            @block.scalar
            def _(act):
                act.wait_ge(consts, 1)

                def body(it):
                    for j in range(U):
                        act.wait_ge(xT_ready, nth(it, j))
                        if not is_first(it):
                            act.wait_ge(mixed, before(it, j))
                        nc.scalar.activation(xT[j][:], pa[j][:, 0:P], ACT.Copy).then_inc(xT_copied, 1)
                    for j in range(U):
                        act.wait_ge(peak_ready, nth(it, j))
                        for half in HALF:
                            last = nc.scalar.activation(E[j][half, half], pb[j][half, 0:S], ACT.Exp, bias=negmax[j][half, :],
                                                        accum_out=total[j][half, :])
                        last.then_inc(exp_ready, 1)
                    for j in range(U):
                        act.wait_ge(ET_ready, nth(it, j))
                        nc.scalar.activation(ET[j][:], pa[j][:, 128:256], ACT.Copy).then_inc(ET_copied, 1)
                    for j in range(U):
                        act.wait_ge(row_ready, nth(it, j))
                        nc.scalar.activation(row[j][:], row[j][:], ACT.Exp).then_inc(row_exp, 1)
                    for j in range(U):
                        act.wait_ge(hq_ready, nth(it, j))
                        nc.scalar.activation(hqT[j][:], pa[j][:, 0:P], ACT.Copy).then_inc(hqT_copied, 1)
                    for j in range(U):
                        act.wait_ge(x2_ready, nth(it, j))
                        nc.scalar.activation(magn[j][:], x2[j][:], ACT.Abs).then_inc(magn_ready, 1)
                    for j in range(U):
                        act.wait_ge(q8T_ready, nth(it, j))
                        nc.scalar.activation(q8T[j][:], pa[j][:, 0:P], ACT.Copy).then_inc(q8T_copied, 1)
                peeled(nc.scalar, steps, body)

            @block.vector
            def _(dve):
                own = Own(dve, dve_own)

                def body(it):
                    own.step(it)
                    for j in range(U):
                        dve.wait_ge(xT_copied, nth(it, j))
                        nc.vector.tensor_scalar(lhs[j][:], xT[j][:], w["w3"][:], w["w2"][:], ALU.mult, ALU.add).then_inc(lhs_ready, 1)
                    marks = []
                    for j in range(U):
                        dve.wait_ge(sim_ready, nth(it, j))
                        marks.append(own.mark(nc.vector.tensor_reduce(peak[j][:], pb[j][:, 0:S], AX, ALU.max)))
                    for j in range(U):
                        own.wait(marks[j])
                        m = own.mark(nc.vector.tensor_scalar(negmax[j][:], peak[j][:], -1.0, None, ALU.mult))
                        own.wait(m)
                        m = own.mark(nc.vector.tensor_scalar(peak[j][:], peak[j][:], w["b_sim"][:], None, ALU.add))
                        own.wait(m)
                        nc.vector.tensor_tensor(peak[j][:], peak[j][:], pb[j][:, S:S + 1], ALU.add).then_inc(peak_ready, 1)
                    for j in range(U):
                        dve.wait_ge(exp_ready, nth(it, j))
                        marks[j] = own.mark(nc.vector.reciprocal(total[j][:], total[j][:]))
                    for j in range(U):
                        own.wait(marks[j])
                        nc.vector.tensor_scalar(E[j][:], E[j][:], total[j][:], None, ALU.mult).then_inc(E_ready, 1)
                    for j in range(U):
                        dve.wait_ge(ET_ready, nth(it, j))
                        dve.wait_ge(ET_copied, nth(it, j))
                        scores = pa[j][0:1, 256:384].rearrange("o (b i) -> o b i", b=2)
                        m = own.mark(nc.vector.tensor_reduce(rowmax[j][:], scores, AX, ALU.max))
                        own.wait(m)
                        nc.vector.tensor_tensor(row[j][:], scores, rowmax[j][:].unsqueeze(2).to_broadcast([1, 2, S]),
                                                ALU.subtract).then_inc(row_ready, 1)
                    for j in range(U):
                        dve.wait_ge(row_exp, nth(it, j))
                        m = own.mark(nc.vector.tensor_reduce(rowmax[j][:], row[j][:], AX, ALU.add))
                        own.wait(m)
                        m = own.mark(nc.vector.reciprocal(rowmax[j][:], rowmax[j][:]))
                        own.wait(m)
                        nc.vector.tensor_tensor(row[j][:], row[j][:], rowmax[j][:].unsqueeze(2).to_broadcast([1, 2, S]),
                                                ALU.mult).then_inc(row_done, 1)
                    for j in range(U):
                        dve.wait_ge(hq_ready, nth(it, j))
                        nc.vector.tensor_copy(bcol[j][:], pb[j][:, 65:66]).then_inc(bcol_copied, 1)
                    for j in range(U):
                        dve.wait_ge(hqT_copied, nth(it, j))
                        nc.vector.tensor_tensor(x_hqT[j][:], xT[j][:], hqT[j][:], ALU.mult)
                        dve.wait_ge(hc_ready, nth(it, j))
                        for b, ps in ((0, pa[j]), (1, pb[j])):
                            last = nc.vector.tensor_scalar(x_hcT[j][:, HALF[b]], xT[j][:, HALF[b]], ps[:, 400:401], None, ALU.mult)
                        last.then_inc(feats_ready, 1)
                    for j in range(U):
                        dve.wait_ge(mixed, nth(it, j))
                        nc.vector.tensor_tensor(y[j][:], pb[j][:, 128:256], x_sb[j][:], ALU.add).then_inc(x_added, 1)
                    norms.stats(nc, own, [t[:] for t in y], EPS_OUT, lambda j: dve.wait_ge(x_added, nth(it, j)))
                    for j in range(U):
                        norms.apply(nc, it, 0, j, y[j][:], x2[j][:]).then_inc(x2_ready, 1)
                    for j in range(U):
                        dve.wait_ge(magn_ready, nth(it, j))
                        marks[j] = own.mark(nc.vector.tensor_reduce(amax[j][:], magn[j][:], AX, ALU.max))
                    for j in range(U):
                        own.wait(marks[j])
                        marks[j] = own.mark(nc.vector.tensor_scalar(amax[j][:], amax[j][:], 1e-5, None, ALU.max))
                    for j in range(U):
                        own.wait(marks[j])
                        nc.vector.tensor_scalar(step8[j][:], amax[j][:], w["scale127"][:], None, ALU.mult)
                        marks[j] = own.mark(nc.vector.reciprocal(total[j][:], amax[j][:]))
                    for j in range(U):
                        own.wait(marks[j])
                        marks[j] = own.mark(nc.vector.tensor_scalar(total[j][:], total[j][:], 127.0, None, ALU.mult))
                    for j in range(U):
                        own.wait(marks[j])
                        marks[j] = own.mark(nc.vector.tensor_scalar(q8[j][:], x2[j][:], total[j][:], ROUND, ALU.mult, ALU.add))
                    for j in range(U):
                        own.wait(marks[j])
                        marks[j] = own.mark(nc.vector.tensor_scalar(q8[j][:], q8[j][:], ROUND, 127.0, ALU.subtract, ALU.min))
                    for j in range(U):
                        own.wait(marks[j])
                        nc.vector.tensor_scalar(q8[j][:], q8[j][:], -128.0, None, ALU.max).then_inc(q8_ready, 1)
                    for j in range(U):
                        dve.wait_ge(ffn_ready, nth(it, j))
                        marks[j] = own.mark(nc.vector.scalar_tensor_tensor(y[j][:], pb[j][:, 0:D], step8[j][:], x2[j][:], ALU.mult, ALU.add))
                    for j in range(U):
                        own.wait(marks[j])
                        marks[j] = own.mark(nc.vector.tensor_tensor(y[j][:], y[j][:], w["ffn_bias"][:], ALU.add))
                    norms.stats(nc, own, [t[:] for t in y], EPS_OUT, lambda j: own.wait(marks[j]))
                    for j in range(U):
                        if not is_first(it):
                            dve.wait_ge(stored[j], 16 * it)
                        norms.apply(nc, it, 1, j, y[j][:], res[j][:]).then_inc(x3_ready, 1)
                peeled(nc.vector, steps, body)


def relative_buckets(rel):
    nb, max_exact, far = 16, 8, 128
    mag = np.abs(rel)
    large = np.log(mag.astype(np.float32) / np.float32(max_exact) + np.float32(1e-6)) / np.float32(np.log(far / max_exact)) * np.float32(nb - max_exact)
    large = np.minimum(max_exact + np.where(mag > 0, large, 0).astype(np.int32), nb - 1)
    return (rel > 0).astype(np.int32) * nb + np.where(mag < max_exact, mag, large)


def setup_attn1(nc, ph, d, ident):
    HD, SPAN = D // H, 256
    SCALE = HD ** -0.5 / 32.0
    w = dict(ident=ident, qkv_w=ph.sb("qkv_w", [D, 3, D]), qkv_b=ph.sb("qkv_b", [P, 3, D]), out_w=ph.sb("out_w", [D, D]),
             out_b=ph.sb("out_b", [P, D]), grep_a=ph.sb("grep_a", [P, H]), neg_gate_b=ph.sb("neg_gate_b", [P, 1]),
             gate_w=ph.sb("gate_w", [P, 4], F16), quarter=ph.sb("quarter", [P, 4]), nth_in_quarter=ph.sb("nth_in_quarter", [H, 4]),
             own_head=ph.sb("own_head", [H, H]), down32=ph.sb("down32", [P, P], F16), ident16=ph.sb("ident16", [P, P], F16), pos=ph.sb("pos", [P, H, B + 1]),
             bias_kv=ph.sb("bias_kv", [P, 2, H], F16))
    skew = nc.dram_tensor("skew", (B, H, SPAN), F32)
    with Phase(nc, "s3") as t:
        onehot, rel, relb = t.sb("onehot", [32, SPAN]), t.sb("rel", [32, H]), t.sb("relb", [32, H, P])
        wide = t.sb("wide", [P, H, SPAN])
        grep_w, grep_b = t.sb("grep_w", [P, 8]), t.sb("grep_b", [P, 8])
        gsum = t.sb("gsum", [P, 1])
        bias32, down32, high_slot, low_slot = t.sb("bias32", [P, 2, H]), t.sb("down32", [P, P]), t.sb("high_slot", [P, 1]), t.sb("low_slot", [P, 1])
        bias_high, bias_low, g_high, g_low = (t.sb("bias_high", [P, 2, H], F16), t.sb("bias_low", [P, 2, H]), t.sb("g_high", [P, 1], F16),
                                              t.sb("g_low", [P, 1]))
        bank = [t.ps(f"bank{i}", [P, 2, SPAN]) for i in range(8)]
        loaded, cleared, relb_ready, spread, wide_ready, skewed, pos_loaded, own_sem = (
            t.sem(n) for n in ("loaded", "cleared", "relb_ready", "spread", "wide_ready", "skewed", "pos_loaded", "own"))
        loads = [(w[k], d[k]) for k in ("qkv_w", "out_w", "quarter", "nth_in_quarter", "own_head")]
        loads += [(w["out_b"], d["out_b"].to_broadcast([P, D])), (w["qkv_b"], d["qkv_b"].to_broadcast([P, 3, D])),
                  (down32, d["down32"]), (high_slot, d["high_slot"]), (low_slot, d["low_slot"]), (onehot, d["onehot"]), (rel, d["rel_emb"]),
                  (grep_b, d["grep_b"].to_broadcast([P, 8])), (w["grep_a"], d["grep_a"].to_broadcast([P, H]))]
        with nc.Block() as block:
            @block.sync
            def _(sp):
                for dst, src in loads:
                    sp.dma_start(dst[:], src[:]).then_inc(loaded, 16)
                sp.wait_ge(cleared, 2)
                for slot in range(3):
                    for a in range(4):
                        at = 32 * a + HD * slot
                        sp.dma_start(grep_w[at:at + HD, :], d["grep_w"][:]).then_inc(loaded, 16)
                    for i, k in enumerate(("bias_kT", "bias_vT")):
                        if slot < 3 - i:
                            sp.dma_start(bias32[96 + HD * slot:96 + HD * (slot + 1), i, :], d[k][:]).then_inc(loaded, 16)
                sp.wait_ge(wide_ready, 1)
                sp.dma_start(skew.ap(), wide[:]).then_inc(skewed, 16)
                sp.wait_ge(skewed, 16)
                shifted = bass.AP(skew, B - 1, [[H * SPAN - 1, B], [SPAN, H], [1, B + 1]])
                sp.dma_start(w["pos"][:], shifted).then_inc(pos_loaded, 16)
                sp.wait_ge(pos_loaded, 16)

            @block.gpsimd
            def _(pool):
                nc.gpsimd.memset(grep_w[:], 0.0).then_inc(cleared, 1)
                nc.gpsimd.memset(bias32[:], 0.0).then_inc(cleared, 1)

            @block.tensor
            def _(pe):
                pe.wait_ge(relb_ready, 1)
                for h in range(H):
                    last = nc.tensor.matmul(bank[h // 2][:, h % 2, :], relb[:, h, :], onehot[:], start=True, stop=True)
                last.then_inc(spread, 1)

            @block.vector
            def _(dve):
                own = Own(dve, own_sem)
                dve.wait_ge(loaded, 16 * (len(loads) + 17))
                nc.vector.tensor_scalar(relb[:], rel[:].unsqueeze(2).to_broadcast([32, H, P]), 1.0 / SCALE, None, ALU.mult).then_inc(relb_ready, 1)
                nc.vector.tensor_copy(w["down32"][:], down32[:])
                nc.vector.tensor_copy(w["ident16"][:], ident[:])
                c = own.mark(nc.vector.tensor_copy(bias_high[:], bias32[:]))
                a = own.mark(nc.vector.tensor_reduce(gsum[:], grep_w[:], AX, ALU.add))
                b = own.mark(nc.vector.tensor_reduce(w["neg_gate_b"][:], grep_b[:], AX, ALU.add))
                own.wait(b)
                nc.vector.tensor_scalar(w["neg_gate_b"][:], w["neg_gate_b"][:], -1.0, None, ALU.mult)
                own.wait(c)
                c = own.mark(nc.vector.tensor_tensor(bias_low[:], bias32[:], bias_high[:], ALU.subtract))
                own.wait(a)
                a = own.mark(nc.vector.tensor_copy(g_high[:], gsum[:]))
                own.wait(a)
                a = own.mark(nc.vector.tensor_tensor(g_low[:], gsum[:], g_high[:], ALU.subtract))
                own.wait(c)
                c = own.mark(nc.vector.tensor_scalar(bias_low[:], bias_low[:], low_slot[:], None, ALU.mult))
                own.wait(a)
                a = own.mark(nc.vector.tensor_tensor(g_low[:], g_low[:], low_slot[:], ALU.mult))
                own.wait(c)
                nc.vector.scalar_tensor_tensor(w["bias_kv"][:].rearrange("p a h -> p (a h)"), bias_high[:].rearrange("p a h -> p (a h)"), high_slot[:],
                                               bias_low[:].rearrange("p a h -> p (a h)"), ALU.mult, ALU.add)
                own.wait(a)
                a = own.mark(nc.vector.scalar_tensor_tensor(g_low[:], g_high[:], high_slot[:], g_low[:], ALU.mult, ALU.add))
                own.wait(a)
                nc.vector.tensor_scalar(w["gate_w"][:], w["quarter"][:], g_low[:], None, ALU.mult)
                dve.wait_ge(spread, 1)
                for i in range(8):
                    last = nc.vector.tensor_copy(wide[:, 2 * i:2 * i + 2, :], bank[i][:])
                last.then_inc(wide_ready, 1)
    return w


def phase_attn1(nc, w, x3, x4):
    U, HD, T, Q, PAD = 4, D // H, B, 4, 32
    ROWS = 32 * H
    KEYS = T + 1
    PARTS = 2 * HD
    SCALE = HD ** -0.5 / 32.0
    steps = S // U
    x3_s = x3.rearrange("(b s) d -> s b d", s=S)
    x4_s = x4.rearrange("(b s) d -> s b d", s=S)

    with Phase(nc, "c") as ph:
        def slots(name, shape, dt=F32):
            return [ph.sb(f"{name}{j}", shape, dt) for j in range(U)]

        x_biased = slots("x_biased", [T, D])
        x_sb, xT = slots("x", [T, D]), slots("xT", [D, T])
        whole = slots("whole", [T, 3, H, HD])
        padded = slots("padded", [T, 3, H, PAD], F16)
        qF = slots("qF", [P, ROWS], F16)
        kvF = slots("kvF", [P, 2, ROWS + H], F16)
        v_sb = slots("v", [T, H, PARTS + 1], F16)
        vlast, vlast_rows = slots("vlast", [P, H]), slots("vlast_rows", [H, H, PARTS + 1])
        sc, p_parts, pT_parts = slots("sc", [T, H, KEYS]), slots("p_parts", [T, 2, H, T], F16), slots("pT_parts", [T, 2, H, T], F16)
        gate, negmax, den = slots("gate", [T, H]), slots("negmax", [T, H]), slots("den", [T, H])
        plastT, attn, attnT = slots("plastT", [H, T]), slots("attn", [T, H, HD]), slots("attnT", [D, T])
        y, res = slots("y", [T, D]), slots("res", [T, D])
        front, back = ph.ps("front", [P, 512]), ph.ps("back", [P, 512])
        sbank = [ph.ps(f"scores{i}", [P, 2, 512]) for i in range(2)]
        tbank = [ph.ps(f"turned{i}", [P, 2, 4, T], F16) for i in range(2)]
        bn, mv = slots("bn", [T, 6]), slots("mv", [T, 2])
        var_eps, rstd, minus_half = slots("var_eps", [T, 1]), slots("rstd", [T, 1]), ph.sb("minus_half", [T, 1])
        loaded = [ph.sem(f"loaded{j}") for j in range(U)]
        stored = [ph.sem(f"stored{j}") for j in range(U)]
        names = ("consts", "xT_ready", "xT_copied", "qkv_ready", "whole_ready", "high_ready", "rows_ready", "z_ready", "gate_exp", "kv_whole",
                 "windows_ready", "v_ready", "vlast_ready", "vrows_turned", "vrows_ready", "gate_done", "scores_ready", "biased",
                 "negmax_ready", "exp_ready", "pT_ready", "p_high_ready", "p_low_ready", "pT_copied", "plast_ready", "plast_copied", "pv_ready", "attn_ready",
                 "attnT_ready", "attnT_copied", "out_ready", "x_added", "x_biased_ready", "var_ready", "rstd_ready", "x4_ready", "own_first",
                 "own_quarters", "own_last", "waited")
        (consts, xT_ready, xT_copied, qkv_ready, whole_ready, high_ready, rows_ready, z_ready, gate_exp, kv_whole, windows_ready, v_ready,
         vlast_ready, vrows_turned, vrows_ready, gate_done, scores_ready, biased, negmax_ready, exp_ready, pT_ready, p_high_ready, p_low_ready, pT_copied,
         plast_ready, plast_copied, pv_ready, attn_ready, attnT_ready, attnT_copied, out_ready, x_added, x_biased_ready, var_ready, rstd_ready, x4_ready,
         own_first, own_quarters, own_last, waited) = (ph.sem(n) for n in names)

        def nth(it, j):
            return U * it + j + 1

        def quarter(it, j, a):
            return Q * U * it + Q * j + a + 1

        def slot(j):
            return j % U

        def is_start(it, j):
            return isinstance(it, int) and U * it + j == 0

        def rounds(it, j):
            return it + j // U + 1

        def pipelined(eng, first, quarters, last):
            def body(it, begins=False, ends=False):
                for j in range(U):
                    quarters(it, j, None if ends and j == U - 1 else (it, j + 1), None if begins and j == 0 else (it, j - 1))
            for part in first:
                part(0, 0)
            body(0, begins=True)
            with eng.Fori(1, steps - 1) as it:
                body(it)
            body(steps - 1, ends=True)
            for part in last:
                part(steps - 1, U - 1)

        def run(part, position):
            if position is not None:
                part(*position)

        def score_cols(a, i):
            return sbank[a % 2][:, i // 2, (i % 2) * KEYS:(i % 2 + 1) * KEYS]

        def first_key(h):
            return KEYS * h - ROWS * (h // 4)

        def query_rows(j, rows, i):
            return qF[j][rows, 128 * i:128 * (i + 1)]

        def last_keys(j):
            ap = kvF[j][:, 1, T:T + 1]
            step = first_key(4) - first_key(0), KEYS
            return bass.AP(ap.tensor, ap.offset, [ap.ap[0], [step[0], 4], [step[1], 4]])

        with nc.Block() as block:
            @block.sync
            def _(sp):
                def body(it):
                    for j in range(U):
                        if not is_first(it):
                            sp.wait_ge(x_added, nth(it, j) - U)
                        sp.dma_start(x_sb[j][:], x3_s[bass.ds(U * it + j, 1)].rearrange("o b d -> (o b) d")).then_inc(loaded[j], 16)
                        if not is_first(it):
                            sp.wait_ge(x4_ready, nth(it, j) - U)
                            sp.dma_start(x4_s[bass.ds(U * it + (j - U), 1)].rearrange("o b d -> (o b) d"), res[j][:]).then_inc(stored[j], 16)
                peeled(nc.sync, steps, body)
                for j in range(U):
                    sp.wait_ge(x4_ready, nth(steps - 1, j))
                    sp.dma_start(x4_s[S - U + j], res[j][:]).then_inc(stored[j], 16)
                for j in range(U):
                    sp.wait_ge(stored[j], 16 * steps)

            @block.gpsimd
            def _(pool):
                for j in range(U):
                    nc.gpsimd.memset(padded[j][:], 0.0)
                    last = nc.gpsimd.memset(v_sb[j][:], 1.0)
                last.then_inc(consts, 1)
                nc.gpsimd.memset(minus_half[:], -0.5).then_inc(consts, 1)
                pool.wait_ge(consts, 2)

                def add_bias(it, j):
                    pool.wait_ge(loaded[slot(j)], 16 * rounds(it, j))
                    if not (isinstance(it, int) and U * it + j < U):
                        pool.wait_ge(x_added, nth(it, j) - U)
                    nc.gpsimd.tensor_tensor(x_biased[slot(j)][:], x_sb[slot(j)][:], w["out_b"][:], ALU.add).then_inc(x_biased_ready, 1)

                def power(it, j):
                    s = slot(j)
                    pool.wait_ge(var_ready, nth(it, j))
                    nc.gpsimd.tensor_tensor(rstd[s][:], var_eps[s][:], minus_half[:], ALU.pow).then_inc(rstd_ready, 1)

                def low(it, j, a):
                    s, hs = slot(j), slice(4 * a, 4 * a + 4)
                    pool.wait_ge(p_high_ready, quarter(it, j, a))
                    nc.gpsimd.tensor_tensor(p_parts[s][:, 1, hs, :], sc[s][:, hs, 0:T], p_parts[s][:, 0, hs, :], ALU.subtract).then_inc(p_low_ready, 1)

                def quarters(it, j, following, previous):
                    low(it, j, 0)
                    low(it, j, 1)
                    low(it, j, 2)
                    run(power, previous)
                    low(it, j, 3)
                    run(add_bias, following)
                pipelined(nc.gpsimd, (add_bias,), quarters, (power,))

            @block.tensor
            def _(pe):
                def turn_x(it, j):
                    pe.wait_ge(loaded[slot(j)], 16 * rounds(it, j))
                    if not is_start(it, j):
                        pe.wait_ge(vrows_ready, nth(it, j) - 1)
                    nc.tensor.transpose(front[:, 0:T], x_sb[slot(j)][:], w["ident"][:]).then_inc(xT_ready, 1)

                def project(it, j):
                    pe.wait_ge(xT_copied, nth(it, j))
                    nc.tensor.matmul(front[:, 0:3 * D], xT[slot(j)][:], w["qkv_w"][:].rearrange("p a e -> p (a e)"),
                                     start=True, stop=True).then_inc(qkv_ready, 1)

                def gates(it, j):
                    pe.wait_ge(rows_ready, nth(it, j))
                    for i in range(4):
                        nc.tensor.matmul(front[:, 4 * i:4 * i + 4], query_rows(slot(j), slice(0, P), i), w["gate_w"][:], start=True, stop=True)
                    nc.tensor.matmul(front[:, 16:48], w["down32"][:], kvF[slot(j)][:, :, 0:H], start=True, stop=True).then_inc(z_ready, 1)

                def windows(it, j):
                    pe.wait_ge(gate_exp, nth(it, j))
                    pe.wait_ge(kv_whole, nth(it, j))
                    for h in range(H):
                        quarter_cols = w["ident16"][:, 32 * (h // 4):32 * (h // 4) + PARTS]
                        last = nc.tensor.matmul(front[:, PARTS * h:PARTS * (h + 1)], kvF[slot(j)][:, 1, first_key(h):first_key(h) + T], quarter_cols,
                                                start=True, stop=True)
                    last.then_inc(windows_ready, 1)

                def turn_last_values(it, j):
                    pe.wait_ge(v_ready, nth(it, j))
                    pe.wait_ge(vlast_ready, nth(it, j))
                    nc.tensor.transpose(front[0:H, 0:P], vlast[slot(j)][:], w["ident"][:]).then_inc(vrows_turned, 1)

                def scores(it, j, a):
                    if a == 0:
                        pe.wait_ge(kv_whole, nth(it, j))
                    if not (is_start(it, j) and a < 2):
                        pe.wait_ge(biased, quarter(it, j, a) - 2)
                    rows = slice(32 * a, 32 * a + 3 * HD)
                    for i in range(4):
                        last = nc.tensor.matmul(score_cols(a, i), query_rows(slot(j), rows, i),
                                                kvF[slot(j)][rows, 0, first_key(4 * a + i):first_key(4 * a + i) + KEYS], start=True, stop=True)
                    last.then_inc(scores_ready, 1)

                def turn(it, j, a):
                    pe.wait_ge(p_low_ready, quarter(it, j, a))
                    if not (is_start(it, j) and a < 2):
                        pe.wait_ge(pT_copied, quarter(it, j, a) - 2)
                    for part in range(2):
                        for i in range(4):
                            last = nc.tensor.transpose(tbank[a % 2][:, part, i, :], p_parts[slot(j)][:, part, 4 * a + i, :], w["ident16"][:])
                    last.then_inc(pT_ready, 1)

                def turn_third(it, j):
                    turn(it, j, 2)

                def turn_last(it, j):
                    turn(it, j, Q - 1)
                    if not is_start(it, j):
                        pe.wait_ge(x_added, nth(it, j) - 1)
                    nc.tensor.transpose(back[0:H, 0:T], sc[slot(j)][:, :, T], w["ident"][:]).then_inc(plast_ready, 1)

                def weigh(it, j):
                    pe.wait_ge(plast_copied, nth(it, j))
                    pe.wait_ge(vrows_ready, nth(it, j))
                    pe.wait_ge(pT_copied, quarter(it, j, Q - 1))
                    out, n = back[:, 128:128 + H * (PARTS + 1)], PARTS + 1
                    nc.tensor.matmul(out, plastT[slot(j)][:], vlast_rows[slot(j)][:].rearrange("n h e -> n (h e)"), start=True, stop=True)
                    for h in range(H):
                        for part in range(2):
                            last = nc.tensor.matmul(out[:, h * n:(h + 1) * n], pT_parts[slot(j)][:, part, h, :], v_sb[slot(j)][:, h, :],
                                                    start=False, stop=True, skip_group_check=True)
                    last.then_inc(pv_ready, 1)

                def turn_attn(it, j):
                    pe.wait_ge(attn_ready, nth(it, j))
                    nc.tensor.transpose(back[:, 0:T], attn[slot(j)][:].rearrange("p h e -> p (h e)"), w["ident"][:]).then_inc(attnT_ready, 1)

                def output(it, j):
                    pe.wait_ge(attnT_copied, nth(it, j))
                    nc.tensor.matmul(back[:, 128:128 + D], attnT[slot(j)][:], w["out_w"][:], start=True, stop=True).then_inc(out_ready, 1)

                def quarters(it, j, following, previous):
                    scores(it, j, 0)
                    run(turn_x, following)
                    run(turn_third, previous)
                    scores(it, j, 1)
                    run(project, following)
                    run(turn_last, previous)
                    scores(it, j, 2)
                    run(weigh, previous)
                    turn(it, j, 0)
                    run(gates, following)
                    scores(it, j, 3)
                    run(turn_attn, previous)
                    turn(it, j, 1)
                    run(windows, following)
                    run(output, previous)
                    run(turn_last_values, following)
                pipelined(nc.tensor, (turn_x, project, gates, windows, turn_last_values), quarters,
                          (turn_third, turn_last, weigh, turn_attn, output))

            @block.scalar
            def _(act):
                def copy_x(it, j):
                    act.wait_ge(xT_ready, nth(it, j))
                    nc.scalar.activation(xT[slot(j)][:], front[:, 0:T], ACT.Copy).then_inc(xT_copied, 1)

                def high_parts(it, j):
                    act.wait_ge(whole_ready, nth(it, j))
                    nc.scalar.activation(padded[slot(j)][:, :, :, 0:HD], whole[slot(j)][:], ACT.Copy).then_inc(high_ready, 1)
                    nc.scalar.activation(padded[slot(j)][:, 0, :, HD:2 * HD], whole[slot(j)][:, 0], ACT.Copy).then_inc(high_ready, 1)
                    nc.scalar.activation(padded[slot(j)][:, 1, :, 2 * HD:3 * HD], whole[slot(j)][:, 1], ACT.Copy).then_inc(high_ready, 1)

                def gates(it, j):
                    act.wait_ge(z_ready, nth(it, j))
                    nc.scalar.activation(gate[slot(j)][:].rearrange("p (a i) -> p i a", a=4), front[:, 0:H].rearrange("p (i a) -> p i a", a=4),
                                         ACT.Exp, bias=w["neg_gate_b"][:], scale=-1.0).then_inc(gate_exp, 1)

                def copy_values(it, j):
                    act.wait_ge(windows_ready, nth(it, j))
                    nc.scalar.activation(v_sb[slot(j)][:, :, 0:PARTS], front[:, 0:H * PARTS].rearrange("p (h e) -> p h e", h=H), ACT.Copy).then_inc(v_ready, 1)

                def exps(it, j, a):
                    act.wait_ge(negmax_ready, quarter(it, j, a))
                    for h in range(4 * a, 4 * a + 4):
                        last = nc.scalar.activation(sc[slot(j)][:, h, :], sc[slot(j)][:, h, :], ACT.Exp, bias=negmax[slot(j)][:, h:h + 1],
                                                    scale=SCALE)
                    last.then_inc(exp_ready, 1)
                    act.wait_ge(exp_ready, quarter(it, j, a))
                    hs = slice(4 * a, 4 * a + 4)
                    nc.scalar.activation(p_parts[slot(j)][:, 0, hs, :], sc[slot(j)][:, hs, 0:T], ACT.Copy).then_inc(p_high_ready, 1)

                def copy_turned(it, j, a):
                    act.wait_ge(pT_ready, quarter(it, j, a))
                    nc.scalar.activation(pT_parts[slot(j)][:, :, 4 * a:4 * a + 4, :], tbank[a % 2][:], ACT.Copy).then_inc(pT_copied, 1)

                def copy_third(it, j):
                    copy_turned(it, j, 2)

                def copy_last(it, j):
                    copy_turned(it, j, Q - 1)
                    act.wait_ge(plast_ready, nth(it, j))
                    nc.scalar.activation(plastT[slot(j)][:], back[0:H, 0:T], ACT.Copy).then_inc(plast_copied, 1)

                def copy_attn(it, j):
                    act.wait_ge(attnT_ready, nth(it, j))
                    nc.scalar.activation(attnT[slot(j)][:], back[:, 0:T], ACT.Copy).then_inc(attnT_copied, 1)

                def quarters(it, j, following, previous):
                    run(copy_x, following)
                    exps(it, j, 0)
                    run(copy_third, previous)
                    exps(it, j, 1)
                    run(copy_last, previous)
                    run(high_parts, following)
                    copy_turned(it, j, 0)
                    exps(it, j, 2)
                    run(gates, following)
                    run(copy_attn, previous)
                    copy_turned(it, j, 1)
                    run(copy_values, following)
                    exps(it, j, 3)
                pipelined(nc.scalar, (copy_x, high_parts, gates, copy_values), quarters, (copy_third, copy_last, copy_attn))

            @block.vector
            def _(dve):
                first_own, quarters_own, last_own = Own(dve, own_first), Own(dve, own_quarters), Own(dve, own_last)
                dve.wait_ge(consts, 1)
                for j in range(U):
                    nc.vector.tensor_copy(kvF[j][96:128, :, ROWS:ROWS + H], w["bias_kv"][96:128, :, :])
                    nc.vector.tensor_copy(vlast_rows[j][:, :, PARTS:PARTS + 1], w["own_head"][:].unsqueeze(2))

                def place(it, j):
                    return j if is_first(it) else U * it + j

                def rows_of_heads(it, j):
                    s, own = slot(j), first_own
                    own.step(place(it, j))
                    dve.wait_ge(qkv_ready, nth(it, j))
                    nc.vector.tensor_tensor(whole[s][:], front[:, 0:3 * D].rearrange("p (a h e) -> p a h e", a=3, h=H),
                                            w["qkv_b"][:].rearrange("p a (h e) -> p a h e", h=H), ALU.add).then_inc(whole_ready, 1)
                    dve.wait_ge(whole_ready, nth(it, j))

                def turn_rows(it, j):
                    s, own = slot(j), first_own
                    dve.wait_ge(high_ready, 3 * nth(it, j))
                    own.mark(nc.vector.tensor_tensor(padded[s][:, 0, :, 2 * HD:3 * HD], whole[s][:, 0], padded[s][:, 0, :, 0:HD], ALU.subtract))
                    m = own.mark(nc.vector.tensor_tensor(padded[s][:, 1:3, :, HD:2 * HD], whole[s][:, 1:3], padded[s][:, 1:3, :, 0:HD], ALU.subtract))
                    own.wait(m)
                    for src, dst in ((0, qF[s][:]), (1, kvF[s][:, 0, 0:ROWS]), (2, kvF[s][:, 1, 0:ROWS])):
                        last = nc.vector.transpose(dst.rearrange("p (t h) -> p h t", h=H), padded[s][:, src])
                    last.then_inc(rows_ready, 1)

                def gates(it, j):
                    s, own = slot(j), first_own
                    dve.wait_ge(z_ready, nth(it, j))
                    dve.wait_ge(gate_exp, nth(it, j))
                    nc.vector.tensor_copy(kvF[s][0:96, :, ROWS:ROWS + H], front[0:96, 16:48].rearrange("p (a h) -> p a h", a=2)).then_inc(kv_whole, 1)
                    m = own.mark(nc.vector.tensor_scalar(gate[s][:], gate[s][:], 1.0, None, ALU.add))
                    dve.wait_ge(kv_whole, nth(it, j))
                    nc.vector.tensor_tensor(vlast[s][:].rearrange("p (a i) -> p a i", a=4), last_keys(s),
                                            w["quarter"][:].unsqueeze(2).to_broadcast([P, 4, 4]), ALU.mult).then_inc(vlast_ready, 1)
                    own.wait(m)
                    m = own.mark(nc.vector.reciprocal(gate[s][:], gate[s][:]))
                    own.wait(m)
                    nc.vector.tensor_tensor(gate[s][:], gate[s][:], w["grep_a"][:], ALU.mult).then_inc(gate_done, 1)

                def last_values(it, j):
                    dve.wait_ge(vrows_turned, nth(it, j))
                    turned = front[0:H, 0:P].rearrange("n (a e) -> n a e", a=4)
                    nc.vector.tensor_tensor(vlast_rows[slot(j)][:, :, 0:PARTS].rearrange("n (a i) e -> n a i e", a=4),
                                            turned[:, :, 0:PARTS].unsqueeze(2).to_broadcast([H, 4, 4, PARTS]),
                                            w["nth_in_quarter"][:].unsqueeze(1).unsqueeze(3).to_broadcast([H, 4, 4, PARTS]),
                                            ALU.mult).then_inc(vrows_ready, 1)

                def bias(it, j, a):
                    s, own = slot(j), quarters_own
                    if a == 0:
                        own.step(place(it, j))
                        dve.wait_ge(gate_done, nth(it, j))
                    hs = slice(4 * a, 4 * a + 4)
                    dve.wait_ge(scores_ready, quarter(it, j, a))
                    for i in range(4):
                        h = 4 * a + i
                        last = nc.vector.scalar_tensor_tensor(sc[s][:, h, :], w["pos"][:, h, :], gate[s][:, h:h + 1],
                                                              score_cols(a, i), ALU.mult, ALU.add)
                    last.then_inc(biased, 1)
                    dve.wait_ge(biased, quarter(it, j, a))
                    m = own.mark(nc.vector.tensor_reduce(negmax[s][:, hs], sc[s][:, hs, :], AX, ALU.max))
                    own.wait(m)
                    nc.vector.tensor_scalar(negmax[s][:, hs], negmax[s][:, hs], -SCALE, None, ALU.mult).then_inc(negmax_ready, 1)

                def normalise(it, j):
                    s, own = slot(j), last_own
                    own.step(place(it, j))
                    dve.wait_ge(pv_ready, nth(it, j))
                    pv = back[:, 128:128 + H * (PARTS + 1)].rearrange("p (h e) -> p h e", h=H)
                    own.mark(nc.vector.reciprocal(den[s][:], pv[:, :, PARTS]))
                    m = own.mark(nc.vector.tensor_reduce(attn[s][:], pv[:, :, 0:PARTS].rearrange("p h (a e) -> p h e a", a=2), AX, ALU.add))
                    own.wait(m)
                    nc.vector.tensor_tensor(attn[s][:], attn[s][:], den[s][:].unsqueeze(2).to_broadcast([T, H, HD]),
                                            ALU.mult).then_inc(attn_ready, 1)

                def add_x(it, j):
                    s, own = slot(j), last_own
                    dve.wait_ge(out_ready, nth(it, j))
                    dve.wait_ge(x_biased_ready, nth(it, j))
                    nc.vector.tensor_tensor(y[s][:], back[:, 128:128 + D], x_biased[s][:], ALU.add).then_inc(x_added, 1)
                    dve.wait_ge(x_added, nth(it, j))
                    m = own.mark(nc.vector.bn_stats(bn[s][:], y[s][:]))
                    own.wait(m)
                    dve.sem_inc(waited, 1)
                    m = own.mark(nc.vector.bn_aggr(mv[s][:], bn[s][:]))
                    own.wait(m)
                    nc.vector.tensor_scalar(var_eps[s][:], mv[s][:, 1:2], EPS_OUT, None, ALU.add).then_inc(var_ready, 1)

                def norm(it, j):
                    s = slot(j)
                    dve.wait_ge(rstd_ready, nth(it, j))
                    if not (isinstance(it, int) and U * it + j < U):
                        dve.wait_ge(stored[s], 16 * (rounds(it, j) - 1))
                    nc.vector.tensor_scalar(res[s][:], y[s][:], mv[s][:, 0:1], rstd[s][:], ALU.subtract, ALU.mult).then_inc(x4_ready, 1)

                def quarters(it, j, following, previous):
                    bias(it, j, 0)
                    bias(it, j, 1)
                    run(rows_of_heads, following)
                    bias(it, j, 2)
                    run(turn_rows, following)
                    run(normalise, previous)
                    bias(it, j, 3)
                    run(gates, following)
                    run(add_x, previous)
                    run(last_values, following)
                    run(norm, previous)
                pipelined(nc.vector, (rows_of_heads, turn_rows, gates, last_values), quarters, (normalise, add_x, norm))


def setup_cross1(nc, ph, d, ident):
    w = dict(ident=ident, Wq=ph.sb("Wq", [D, D]), Wk=ph.sb("Wk", [D, D]), Wo=ph.sb("Wo", [D, D]), variant=ph.sb("variant", [D, 4]),
             router=ph.sb("router", [D, 64]), e_bias=ph.sb("e_bias", [P, 64]))
    with Phase(nc, "s4") as t:
        loaded = t.sem("loaded")
        loads = [(w[k], d[k]) for k in ("Wq", "Wk", "Wo", "variant", "router")] + [(w["e_bias"], d["e_bias"].to_broadcast([P, 64]))]
        with nc.Block() as block:
            @block.sync
            def _(sp):
                for dst, src in loads:
                    sp.dma_start(dst[:], src[:]).then_inc(loaded, 16)
                sp.wait_ge(loaded, 16 * len(loads))
    return w


def phase_cross1(nc, w, x4, ctx, ctxT, x5, x5T):
    U, HD, PAIRS = 2, D // H, H // 2
    HALF = [slice(0, S), slice(S, 2 * S)]
    steps = TILES // U

    with Phase(nc, "d1") as ph:
        def slots(name, shape):
            return [ph.sb(f"{name}{j}", shape) for j in range(U)]

        x_sb, x_again, cT_sb, cT2 = slots("x", [P, D]), slots("x_again", [P, D]), slots("cT", [D, P]), slots("cT2", [D, 2, 2, S])
        xT, qT, kT, kB = slots("xT", [D, P]), slots("qT", [D, P]), slots("kT", [D, P]), slots("kB", [D, 4, P])
        vB = [[ph.sb(f"vB{j}{b}", [P, PAIRS, 2, HD + 1]) for b in range(2)] for j in range(U)]
        e_sb, eT = slots("e", [P, H, S]), slots("eT", [P, PAIRS, P])
        top, den, attn, attnT = slots("top", [P, H]), slots("den", [P, H]), slots("attn", [P, H, HD]), slots("attnT", [D, P])
        y, res, resT = slots("y", [P, D]), slots("res", [P, D]), slots("resT", [D, P])
        bank = [ph.ps(f"bank{j}", [P, 4, 512]) for j in range(U)]
        norms = Norms(ph, U, 1)
        loaded = [ph.sem(f"loaded{j}") for j in range(U)]
        loaded_again = [ph.sem(f"loaded_again{j}") for j in range(U)]
        stored = [ph.sem(f"stored{j}") for j in range(U)]
        names = ("consts", "xT_ready", "xT_copied", "cT2_ready", "qk_ready", "q_copied", "k_copied", "kB_ready", "vB_ready", "scores_ready",
                 "shifted", "exp_ready", "eT_ready", "eT_copied", "pv_ready", "attn_ready", "attnT_ready", "attnT_copied", "out_ready",
                 "x_added", "x5_ready", "x5T_ready", "x5T_copied", "dve_own", "waited")
        (consts, xT_ready, xT_copied, cT2_ready, qk_ready, q_copied, k_copied, kB_ready, vB_ready, scores_ready,
         shifted, exp_ready, eT_ready, eT_copied, pv_ready, attn_ready, attnT_ready, attnT_copied, out_ready,
         x_added, x5_ready, x5T_ready, x5T_copied, dve_own, waited) = (ph.sem(n) for n in names)

        def nth(it, j):
            return U * it + j + 1

        def before(it, j):
            return U * it + (j + 1 - U)

        def store(sp, j, rows, cols):
            sp.dma_start(x5[rows, :], res[j][:]).then_inc(stored[j], 16)
            sp.dma_start(x5T[:, cols], resT[j][:]).then_inc(stored[j], 16)

        def ahead(eng, front, body):
            for part in front:
                part(0)
            body(0, lambda part: part(1), lambda part: None)
            with eng.Fori(1, steps - 1) as it:
                body(it, lambda part: part(it + 1), lambda part: part(it - 1))
            body(steps - 1, lambda part: None, lambda part: part(steps - 2))

        with nc.Block() as block:
            @block.sync
            def _(sp):
                def body(it):
                    for j in range(U):
                        tile = bass.ds((U * it + j) * P, P)
                        if not is_first(it):
                            sp.wait_ge(qk_ready, before(it, j))
                        sp.dma_start(x_sb[j][:], x4[tile, :]).then_inc(loaded[j], 16)
                        sp.dma_start(cT_sb[j][:], ctxT[:, tile]).then_inc(loaded[j], 16)
                    for j in range(U):
                        if not is_first(it):
                            sp.wait_ge(x_added, before(it, j))
                        sp.dma_start(x_again[j][:], x4[bass.ds((U * it + j) * P, P), :]).then_inc(loaded_again[j], 16)
                    if not is_first(it):
                        for j in range(U):
                            tile = bass.ds((U * it + (j - U)) * P, P)
                            sp.wait_ge(x5T_copied, before(it, j))
                            store(sp, j, tile, tile)
                peeled(nc.sync, steps, body)
                for j in range(U):
                    tile = slice((TILES - U + j) * P, (TILES - U + j + 1) * P)
                    sp.wait_ge(x5T_copied, nth(steps - 1, j))
                    store(sp, j, tile, tile)
                for j in range(U):
                    sp.wait_ge(stored[j], 32 * steps)

            @block.gpsimd
            def _(pool):
                for j in range(U):
                    for b in range(2):
                        nc.gpsimd.memset(vB[j][b][:], 0.0).then_inc(consts, 1)
                norms.setup_power(nc)
                peeled(nc.gpsimd, steps, lambda it: norms.power(nc, it, 0))

            @block.tensor
            def _(pe):
                def turn_x(it):
                    for j in range(U):
                        pe.wait_ge(loaded[j], 32 * (it + 1))
                        nc.tensor.transpose(bank[j][:, 0, 0:P], x_sb[j][:], w["ident"][:]).then_inc(xT_ready, 1)

                def project(it):
                    for j in range(U):
                        pe.wait_ge(xT_copied, nth(it, j))
                        pe.wait_ge(cT2_ready, nth(it, j))
                        if not is_first(it):
                            pe.wait_ge(attn_ready, before(it, j))
                        nc.tensor.matmul(bank[j][:, 0, 128:256], w["Wq"][:], xT[j][:], start=True, stop=True)
                        nc.tensor.matmul(bank[j][:, 1, 0:P], w["Wk"][:], cT_sb[j][:], start=True, stop=True)
                        for b in range(2):
                            last = nc.tensor.matmul(bank[j][:, 2, b * D:(b + 1) * D], cT2[j][:, b].rearrange("d a m -> d (a m)"), w["Wk"][:],
                                                    start=True, stop=True)
                        last.then_inc(qk_ready, 1)

                def turn_result(it, next_scores_read):
                    for j in range(U):
                        pe.wait_ge(x5_ready, nth(it, j))
                        if next_scores_read:
                            pe.wait_ge(shifted, nth(it, j) + U)
                        nc.tensor.transpose(bank[j][:, 3, 0:P], res[j][:], w["ident"][:]).then_inc(x5T_ready, 1)

                def body(it, following, previous):
                    for j in range(U):
                        pe.wait_ge(q_copied, nth(it, j))
                        pe.wait_ge(kB_ready, nth(it, j))
                        pe.wait_ge(vB_ready, nth(it, j))
                        pe.sem_inc(waited, 1)
                        for g in range(4):
                            rows = slice(32 * g, 32 * g + 32)
                            for half in HALF:
                                last = nc.tensor.matmul(bank[j][half, g, 0:4 * S], qT[j][rows, half], kB[j][rows, :, half],
                                                        start=True, stop=True)
                        last.then_inc(scores_ready, 1)
                    previous(lambda before: turn_result(before, True))
                    for j in range(U):
                        pe.wait_ge(exp_ready, nth(it, j))
                        for q in range(PAIRS):
                            last = nc.tensor.transpose(bank[j][:, q // 4, (q % 4) * P:(q % 4 + 1) * P],
                                                       e_sb[j][:, 2 * q:2 * q + 2, :].rearrange("p h m -> p (h m)"), w["ident"][:])
                        last.then_inc(eT_ready, 1)
                    for j in range(U):
                        pe.wait_ge(eT_copied, nth(it, j))
                        for b in range(2):
                            for q in range(PAIRS):
                                cols = slice(q * 2 * (HD + 1), (q + 1) * 2 * (HD + 1))
                                last = nc.tensor.matmul(bank[j][HALF[b], 2, cols], eT[j][:, q, HALF[b]],
                                                        vB[j][b][:, q].rearrange("p a e -> p (a e)"), start=True, stop=True)
                        last.then_inc(pv_ready, 1)
                    following(turn_x)
                    for j in range(U):
                        pe.wait_ge(attn_ready, nth(it, j))
                        if not is_first(it):
                            pe.wait_ge(x5T_copied, before(it, j))
                        nc.tensor.transpose(bank[j][:, 3, 0:P], attn[j][:].rearrange("p h e -> p (h e)"), w["ident"][:]).then_inc(attnT_ready, 1)
                    for j in range(U):
                        pe.wait_ge(attnT_copied, nth(it, j))
                        nc.tensor.matmul(bank[j][:, 3, 128:256], attnT[j][:], w["Wo"][:], start=True, stop=True).then_inc(out_ready, 1)
                    following(project)
                ahead(nc.tensor, (turn_x, project), body)
                turn_result(steps - 1, False)

            @block.scalar
            def _(act):
                def copy_x(it):
                    for j in range(U):
                        act.wait_ge(xT_ready, nth(it, j))
                        nc.scalar.activation(xT[j][:], bank[j][:, 0, 0:P], ACT.Copy).then_inc(xT_copied, 1)

                def copy_qk(it):
                    for j in range(U):
                        act.wait_ge(qk_ready, nth(it, j))
                        nc.scalar.activation(qT[j][:], bank[j][:, 0, 128:256], ACT.Copy, scale=HD ** -0.5).then_inc(q_copied, 1)
                        nc.scalar.activation(kT[j][:], bank[j][:, 1, 0:P], ACT.Copy).then_inc(k_copied, 1)

                def copy_result(it):
                    for j in range(U):
                        act.wait_ge(x5T_ready, nth(it, j))
                        if not is_first(it):
                            act.wait_ge(stored[j], 32 * it)
                        nc.scalar.activation(resT[j][:], bank[j][:, 3, 0:P], ACT.Copy).then_inc(x5T_copied, 1)

                def body(it, following, previous):
                    for j in range(U):
                        act.wait_ge(shifted, nth(it, j))
                        nc.scalar.activation(e_sb[j][:], e_sb[j][:], ACT.Exp).then_inc(exp_ready, 1)
                    previous(copy_result)
                    for j in range(U):
                        act.wait_ge(eT_ready, nth(it, j))
                        nc.scalar.activation(eT[j][:].rearrange("p (g q) t -> p g (q t)", g=2), bank[j][:, 0:2, :], ACT.Copy).then_inc(eT_copied, 1)
                    following(copy_x)
                    for j in range(U):
                        act.wait_ge(attnT_ready, nth(it, j))
                        nc.scalar.activation(attnT[j][:], bank[j][:, 3, 0:P], ACT.Copy).then_inc(attnT_copied, 1)
                    following(copy_qk)
                ahead(nc.scalar, (copy_x, copy_qk), body)
                copy_result(steps - 1)

            @block.vector
            def _(dve):
                own = Own(dve, dve_own)
                dve.wait_ge(consts, 2 * U)
                for j in range(U):
                    for b in range(2):
                        for hh in range(2):
                            nc.vector.memset(vB[j][b][HALF[hh], :, hh, HD:HD + 1], 1.0)

                def double_context(it):
                    for j in range(U):
                        dve.wait_ge(loaded[j], 32 * (it + 1))
                        nc.vector.tensor_copy(cT2[j][:], cT_sb[j][:].rearrange("d (b m) -> d b m", b=2).unsqueeze(2).to_broadcast([D, 2, 2, S])
                                              ).then_inc(cT2_ready, 1)

                def spread_keys(it):
                    for j in range(U):
                        dve.wait_ge(k_copied, nth(it, j))
                        nc.vector.tensor_tensor(kB[j][:], kT[j][:].unsqueeze(1).to_broadcast([D, 4, P]),
                                                w["variant"][:].unsqueeze(2).to_broadcast([D, 4, P]), ALU.mult).then_inc(kB_ready, 1)
                        for b in range(2):
                            keys = bank[j][:, 2, b * D:(b + 1) * D].rearrange("p (q a e) -> p q a e", q=PAIRS, a=2)
                            for hh in range(2):
                                last = nc.vector.tensor_copy(vB[j][b][HALF[hh], :, hh, 0:HD], keys[HALF[hh], :, hh, :])
                        last.then_inc(vB_ready, 1)

                def body(it, following, previous):
                    own.step(it)
                    for j in range(U):
                        dve.wait_ge(scores_ready, nth(it, j))
                        scores = bank[j][:, :, 0:4 * S].rearrange("p g (i m) -> p g i m", i=4)
                        m = own.mark(nc.vector.tensor_reduce(top[j][:].rearrange("p (g i) -> p g i", g=4), scores, AX, ALU.max))
                        own.wait(m)
                        nc.vector.tensor_tensor(e_sb[j][:].rearrange("p (g i) m -> p g i m", g=4), scores,
                                                top[j][:].rearrange("p (g i) -> p g i", g=4).unsqueeze(3).to_broadcast([P, 4, 4, S]),
                                                ALU.subtract).then_inc(shifted, 1)
                    following(double_context)
                    for j in range(U):
                        dve.wait_ge(pv_ready, nth(it, j))
                        pv = bank[j][:, 2, 0:H * (HD + 1)].rearrange("p (h e) -> p h e", h=H)
                        m = own.mark(nc.vector.reciprocal(den[j][:], pv[:, :, HD]))
                        own.wait(m)
                        nc.vector.tensor_tensor(attn[j][:], pv[:, :, 0:HD], den[j][:].unsqueeze(2).to_broadcast([P, H, HD]),
                                                ALU.mult).then_inc(attn_ready, 1)
                    for j in range(U):
                        dve.wait_ge(out_ready, nth(it, j))
                        dve.wait_ge(loaded_again[j], 16 * (it + 1))
                        nc.vector.tensor_tensor(y[j][:], bank[j][:, 3, 128:256], x_again[j][:], ALU.add).then_inc(x_added, 1)
                    norms.stats(nc, own, [t[:] for t in y], EPS_OUT, lambda j: dve.wait_ge(x_added, nth(it, j)))
                    following(spread_keys)
                    for j in range(U):
                        if not is_first(it):
                            dve.wait_ge(stored[j], 32 * it)
                        norms.apply(nc, it, 0, j, y[j][:], res[j][:]).then_inc(x5_ready, 1)
                ahead(nc.vector, (double_context, spread_keys), body)



def phase_router(nc, w, x5T, coefT):
    U, N, E, G = 2, 8, 64, 8
    SCALE, CHOSEN, NONE_LEFT = 2.5, -3.0e38, -1.0e38
    steps = TILES // (U * N)

    with Phase(nc, "rt") as ph:
        def slots(name, shape):
            return [ph.sb(f"{name}{j}", shape) for j in range(U)]

        xT, coefT_sb = slots("xT", [D, N * P]), slots("coefT", [E, N * P])
        score, biased, left, coef = (slots(n, [P, N, E]) for n in ("score", "biased", "left", "coef"))
        best2, groups, gtop, gleft = slots("best2", [P, N, G, 8]), slots("groups", [P, N, G + 4]), slots("gtop", [P, N, 8]), slots("gleft", [P, N, G + 4])
        etop, total = slots("etop", [P, N, 8]), slots("total", [P, N])
        logits = [ph.ps(f"logits{j}", [P, N, E]) for j in range(U)]
        turned = [ph.ps(f"turned{j}", [E, N * P]) for j in range(U)]
        loaded = [ph.sem(f"loaded{j}") for j in range(U)]
        stored = [ph.sem(f"stored{j}") for j in range(U)]
        (consts, logits_ready, logits_exp, coef_ready, coefT_ready, coefT_copied, dve_own, waited) = (ph.sem(n) for n in (
            "consts", "logits_ready", "logits_exp", "coef_ready", "coefT_ready", "coefT_copied", "dve_own", "waited"))

        def nth(it, j):
            return U * it + j + 1

        def before(it, j):
            return U * it + (j + 1 - U)

        with nc.Block() as block:
            @block.sync
            def _(sp):
                def body(it):
                    for j in range(U):
                        if not is_first(it):
                            sp.wait_ge(logits_ready, before(it, j))
                        sp.dma_start(xT[j][:], x5T[:, bass.ds((U * it + j) * N * P, N * P)]).then_inc(loaded[j], 16)
                    if not is_first(it):
                        for j in range(U):
                            sp.wait_ge(coefT_copied, before(it, j))
                            sp.dma_start(coefT[:, bass.ds((U * it + (j - U)) * N * P, N * P)], coefT_sb[j][:]).then_inc(stored[j], 16)
                peeled(nc.sync, steps, body)
                for j in range(U):
                    sp.wait_ge(coefT_copied, nth(steps - 1, j))
                    sp.dma_start(coefT[:, TOK - (U - j) * N * P:TOK - (U - j - 1) * N * P], coefT_sb[j][:]).then_inc(stored[j], 16)
                for j in range(U):
                    sp.wait_ge(stored[j], 16 * steps)

            @block.gpsimd
            def _(pool):
                for j in range(U):
                    nc.gpsimd.memset(groups[j][:, :, G:G + 4], 1.0e30).then_inc(consts, 1)

            @block.tensor
            def _(pe):
                def body(it):
                    for j in range(U):
                        pe.wait_ge(loaded[j], 16 * (it + 1))
                        if not is_first(it):
                            pe.wait_ge(logits_exp, before(it, j))
                        for n in range(N):
                            last = nc.tensor.matmul(logits[j][:, n, :], xT[j][:, n * P:(n + 1) * P], w["router"][:], start=True, stop=True)
                        last.then_inc(logits_ready, 1)
                    for j in range(U):
                        pe.wait_ge(coef_ready, nth(it, j))
                        if not is_first(it):
                            pe.wait_ge(coefT_copied, before(it, j))
                        pe.sem_inc(waited, 1)
                        for n in range(N):
                            last = nc.tensor.transpose(turned[j][:, n * P:(n + 1) * P], coef[j][:, n, :], w["ident"][:])
                        last.then_inc(coefT_ready, 1)
                peeled(nc.tensor, steps, body)

            @block.scalar
            def _(act):
                def body(it):
                    for j in range(U):
                        act.wait_ge(logits_ready, nth(it, j))
                        if not is_first(it):
                            act.wait_ge(coef_ready, before(it, j))
                        nc.scalar.activation(score[j][:], logits[j][:], ACT.Exp, scale=-1.0).then_inc(logits_exp, 1)
                    for j in range(U):
                        act.wait_ge(coefT_ready, nth(it, j))
                        if not is_first(it):
                            act.wait_ge(stored[j], 16 * it)
                        nc.scalar.activation(coefT_sb[j][:], turned[j][:], ACT.Copy).then_inc(coefT_copied, 1)
                peeled(nc.scalar, steps, body)

            @block.vector
            def _(dve):
                own = Own(dve, dve_own)
                dve.wait_ge(consts, U)

                def body(it):
                    own.step(it)
                    marks = [None] * U

                    def stage(op):
                        for j in range(U):
                            own.wait(marks[j])
                            marks[j] = own.mark(op(j))

                    def of_each(op, *ranges):
                        dve.sem_inc(waited, 1)
                        for index in np.ndindex(*ranges):
                            last = op(*(int(i) for i in index))
                        return last

                    for j in range(U):
                        dve.wait_ge(logits_exp, nth(it, j))
                        marks[j] = own.mark(nc.vector.tensor_scalar(score[j][:], score[j][:], 1.0, None, ALU.add))
                    stage(lambda j: nc.vector.reciprocal(score[j][:], score[j][:]))
                    stage(lambda j: nc.vector.tensor_tensor(biased[j][:], score[j][:], w["e_bias"][:].unsqueeze(1).to_broadcast([P, N, E]), ALU.add))
                    stage(lambda j: of_each(lambda n, g: nc.vector.max(best2[j][:, n, g, :], biased[j][:, n, 8 * g:8 * g + 8]), N, G))
                    stage(lambda j: nc.vector.tensor_tensor(groups[j][:, :, 0:G], best2[j][:, :, :, 0], best2[j][:, :, :, 1], ALU.add))
                    stage(lambda j: of_each(lambda n: nc.vector.max(gtop[j][:, n, :], groups[j][:, n, :]), N))
                    stage(lambda j: of_each(lambda n: nc.vector.match_replace(gleft[j][:, n, :], gtop[j][:, n, :], groups[j][:, n, :], CHOSEN), N))
                    stage(lambda j: nc.vector.tensor_scalar(gleft[j][:], gleft[j][:], NONE_LEFT, None, ALU.is_lt))
                    stage(lambda j: nc.vector.tensor_tensor(biased[j][:].rearrange("p n (g e) -> p n g e", g=G), biased[j][:].rearrange("p n (g e) -> p n g e", g=G),
                                                            gleft[j][:, :, 0:G].unsqueeze(3).to_broadcast([P, N, G, 8]), ALU.mult))
                    stage(lambda j: of_each(lambda n: nc.vector.max(etop[j][:, n, :], biased[j][:, n, :]), N))
                    stage(lambda j: of_each(lambda n: nc.vector.match_replace(left[j][:, n, :], etop[j][:, n, :], biased[j][:, n, :], CHOSEN), N))
                    stage(lambda j: nc.vector.scalar_tensor_tensor(left[j][:].rearrange("p n e -> p (n e)"), left[j][:].rearrange("p n e -> p (n e)"), NONE_LEFT,
                                                                   score[j][:].rearrange("p n e -> p (n e)"), ALU.is_lt, ALU.mult))
                    stage(lambda j: nc.vector.tensor_reduce(total[j][:], left[j][:], AX, ALU.add))
                    stage(lambda j: nc.vector.tensor_scalar(total[j][:], total[j][:], 1e-20, None, ALU.add))
                    stage(lambda j: nc.vector.reciprocal(total[j][:], total[j][:]))
                    stage(lambda j: nc.vector.tensor_scalar(total[j][:], total[j][:], SCALE, None, ALU.mult))
                    for j in range(U):
                        own.wait(marks[j])
                        nc.vector.tensor_tensor(coef[j][:], left[j][:], total[j][:].unsqueeze(2).to_broadcast([P, N, E]), ALU.mult).then_inc(coef_ready, 1)
                peeled(nc.vector, steps, body)


PAIRS_E = 32
UNITS = PAIRS_E + 1
W_SCALE, H_SCALE = 256.0, 16.0


def setup_moe(nc, ph, d, ident):
    w = dict(ident=ident, pick=ph.sb("pick", [64, 16, P], F16))
    for k in ("Wg", "Wu", "Wd"):
        w[k] = [ph.sb(f"{k}_{part}", [P, UNITS, P], F16) for part in ("high", "low")]
    CHUNK, BUFS = 11, 3
    work = [(k, c) for k in ("Wg", "Wu", "Wd") for c in range(0, UNITS, CHUNK)]
    with Phase(nc, "s5") as t:
        stage = [t.sb(f"stage{i}", [P, CHUNK, P]) for i in range(BUFS)]
        pick32 = t.sb("pick32", [64, 16, P])
        loaded = [t.sem(f"loaded{i}") for i in range(BUFS)]
        pick_loaded, high_ready, low_ready = t.sem("pick_loaded"), t.sem("high_ready"), t.sem("low_ready")
        with nc.Block() as block:
            @block.sync
            def _(sp):
                sp.dma_start(pick32[:], d["pick"][:]).then_inc(pick_loaded, 16)
                for n, (k, c) in enumerate(work):
                    if n >= BUFS:
                        sp.wait_ge(low_ready, n - BUFS + 1)
                    sp.dma_start(stage[n % BUFS][:], d[k][:, c:c + CHUNK, :]).then_inc(loaded[n % BUFS], 16)

            @block.scalar
            def _(act):
                act.wait_ge(pick_loaded, 16)
                nc.scalar.activation(w["pick"][:], pick32[:], ACT.Copy, scale=1.0 / H_SCALE)
                for n, (k, c) in enumerate(work):
                    act.wait_ge(loaded[n % BUFS], 16 * (n // BUFS + 1))
                    nc.scalar.activation(w[k][0][:, c:c + CHUNK, :], stage[n % BUFS][:], ACT.Copy, scale=W_SCALE).then_inc(high_ready, 1)

            @block.vector
            def _(dve):
                for n, (k, c) in enumerate(work):
                    dve.wait_ge(high_ready, n + 1)
                    nc.vector.scalar_tensor_tensor(w[k][1][:, c:c + CHUNK, :].rearrange("p u n -> p (u n)"), stage[n % BUFS][:].rearrange("p u n -> p (u n)"),
                                                   W_SCALE, w[k][0][:, c:c + CHUNK, :].rearrange("p u n -> p (u n)"),
                                                   ALU.mult, ALU.subtract).then_inc(low_ready, 1)
    return w


def phase_moe(nc, w, x5, x5T, coefT, out):
    U, GROUP, LAG, TAIL = 2, 512, 3, 5
    QT = GROUP // P
    steps = TOK // (GROUP * U)

    with Phase(nc, "d2") as ph:
        def slots(name, shape, dt=F32):
            return [ph.sb(f"{name}{j}", shape, dt) for j in range(U)]

        x_sb, xT, coefs = slots("x", [P, QT, D]), slots("xT", [D, GROUP]), slots("coefs", [64, 2, GROUP])
        x_high, x_low, c_parts = slots("x_high", [D, GROUP], F16), slots("x_low", [D, GROUP], F16), slots("c_parts", [64, 2, GROUP], F16)
        NB = 6
        gated = [ph.sb(f"gated{i}", [P, GROUP]) for i in range(NB)]
        hidden = [ph.sb(f"hidden{i}", [P, GROUP]) for i in range(NB)]
        h_high = [ph.sb(f"h_high{i}", [P, GROUP], F16) for i in range(NB)]
        h_low = [ph.sb(f"h_low{i}", [P, GROUP], F16) for i in range(NB)]
        oT, y, res = slots("oT", [D, GROUP]), slots("y", [P, QT, D]), slots("res", [P, QT, D])
        bn, mv = slots("bn", [P, QT, 6]), slots("mv", [P, QT, 2])
        var_eps, rstd = slots("var_eps", [P, QT]), slots("rstd", [P, QT])
        minus_half = ph.sb("minus_half", [P, QT])
        ps_g = [ph.ps(f"g{i}", [P, GROUP]) for i in range(2)]
        ps_u = [ph.ps(f"u{i}", [P, GROUP]) for i in range(2)]
        ps_c = [ph.ps(f"c{i}", [P, GROUP]) for i in range(2)]
        ps_o = [ph.ps(f"o{j}", [P, GROUP]) for j in range(U)]
        loaded = [ph.sem(f"loaded{j}") for j in range(U)]
        stored = [ph.sem(f"stored{j}") for j in range(U)]
        names = ("consts", "x_high_ready", "c_high_ready", "x_low_ready", "c_low_ready", "guc_ready", "silu_ready", "h_ready", "h_high_ready",
                 "h_low_ready", "down_done", "oT_copied", "turned", "x_added", "var_ready", "rstd_ready", "y_ready", "dve_own", "waited")
        (consts, x_high_ready, c_high_ready, x_low_ready, c_low_ready, guc_ready, silu_ready, h_ready, h_high_ready,
         h_low_ready, down_done, oT_copied, turned, x_added, var_ready, rstd_ready, y_ready, dve_own, waited) = (
            ph.sem(n) for n in names)

        def nth(it, j):
            return U * it + j + 1

        def before(it, j):
            return U * it + (j + 1 - U)

        def unit(it, j, u):
            return UNITS * U * it + UNITS * j + u + 1

        def after(eng, sem, it, j, u, back):
            if not (is_first(it) and UNITS * j + u < back):
                eng.wait_ge(sem, unit(it, j, u) - back)

        def pos(j, u):
            return UNITS * j + u

        assert (UNITS * U) % NB == 0 and (UNITS * U) % 2 == 0

        def rows(dram, at):
            return dram[at, :].rearrange("(q p) d -> p q d", p=P)

        with nc.Block() as block:
            @block.sync
            def _(sp):
                def body(it):
                    for j in range(U):
                        cols = bass.ds((U * it + j) * GROUP, GROUP)
                        if not is_first(it):
                            sp.wait_ge(x_added, before(it, j))
                            sp.wait_ge(x_low_ready, before(it, j))
                            sp.wait_ge(c_low_ready, before(it, j))
                        sp.dma_start(xT[j][:], x5T[:, cols]).then_inc(loaded[j], 16)
                        for part in range(2):
                            sp.dma_start(coefs[j][32 * part:32 * part + 32], coefT[:, cols].rearrange("(a e) t -> e a t", a=2)).then_inc(loaded[j], 16)
                        sp.dma_start(x_sb[j][:], rows(x5, cols)).then_inc(loaded[j], 16)
                        if not is_first(it):
                            sp.wait_ge(y_ready, before(it, j))
                            sp.dma_start(rows(out, bass.ds((U * it + (j - U)) * GROUP, GROUP)), res[j][:]).then_inc(stored[j], 16)
                peeled(nc.sync, steps, body)
                for j in range(U):
                    sp.wait_ge(y_ready, nth(steps - 1, j))
                    sp.dma_start(rows(out, slice(TOK - (U - j) * GROUP, TOK - (U - j - 1) * GROUP)), res[j][:]).then_inc(stored[j], 16)
                for j in range(U):
                    sp.wait_ge(stored[j], 16 * steps)

            @block.gpsimd
            def _(pool):
                nc.gpsimd.memset(minus_half[:], -0.5).then_inc(consts, 1)
                pool.wait_ge(consts, 1)

                def power(it, j):
                    pool.wait_ge(var_ready, nth(it, j))
                    nc.gpsimd.tensor_tensor(rstd[j][:], var_eps[j][:], minus_half[:], ALU.pow).then_inc(rstd_ready, 1)

                def body(it):
                    for j in range(U):
                        pool.wait_ge(x_high_ready, nth(it, j))
                        if not is_first(it):
                            pool.wait_ge(down_done, unit(it, j, UNITS - 1) - UNITS * U)
                        nc.gpsimd.tensor_tensor(x_low[j][:], xT[j][:], x_high[j][:], ALU.subtract).then_inc(x_low_ready, 1)
                        pool.wait_ge(c_high_ready, nth(it, j))
                        pool.wait_ge(x_low_ready, nth(it, j))
                        nc.gpsimd.tensor_tensor(c_parts[j][32:64], coefs[j][32:64], c_parts[j][32:64], ALU.subtract).then_inc(c_low_ready, 1)
                        pool.wait_ge(c_low_ready, nth(it, j))
                    for j in range(U):
                        power(it, j)
                peeled(nc.gpsimd, steps, body)

            @block.tensor
            def _(pe):
                def thrice(out, weights, high, low, start, stop):
                    nc.tensor.matmul(out, weights[0], high, start=start, stop=False)
                    nc.tensor.matmul(out, weights[1], high, start=False, stop=False)
                    return nc.tensor.matmul(out, weights[0], low, start=False, stop=stop)

                def up(it, j, u):
                    i = pos(j, u) % 2
                    after(pe, h_ready, it, j, u, 2)
                    for name, bank in (("Wg", ps_g), ("Wu", ps_u)):
                        last = thrice(bank[i][:], [part[:, u, :] for part in w[name]], x_high[j][:], x_low[j][:], True, True)
                    if u < PAIRS_E:
                        last = nc.tensor.matmul(ps_c[i][:], w["pick"][:, u % 16, :], c_parts[j][:, u // 16, :], start=True, stop=True)
                    last.then_inc(guc_ready, 1)

                def down(it, j, u):
                    b = pos(j, u) % NB
                    pe.wait_ge(h_high_ready, unit(it, j, u))
                    pe.wait_ge(h_low_ready, unit(it, j, u))
                    last = thrice(ps_o[j][:], [part[:, u, :] for part in w["Wd"]], h_high[b][:], h_low[b][:], u == 0, u == UNITS - 1)
                    last.then_inc(down_done, 1)

                def tail(it, j):
                    pe.wait_ge(oT_copied, nth(it, j))
                    for q in range(QT):
                        last = nc.tensor.transpose(ps_o[j][:, q * P:(q + 1) * P], oT[j][:, q * P:(q + 1) * P], w["ident"][:])
                    last.then_inc(turned, 1)

                def body(it):
                    for j in range(U):
                        pe.wait_ge(x_low_ready, nth(it, j))
                        pe.wait_ge(c_low_ready, nth(it, j))
                        if not is_first(it):
                            pe.wait_ge(x_added, before(it, j))
                        for u in range(UNITS + LAG):
                            if u < UNITS:
                                up(it, j, u)
                            if u >= LAG:
                                down(it, j, u - LAG)
                            if j and u == TAIL:
                                tail(it, j - 1)
                    tail(it, U - 1)
                peeled(nc.tensor, steps, body)

            @block.scalar
            def _(act):
                def body(it):
                    for j in range(U):
                        act.wait_ge(loaded[j], 64 * (it + 1))
                        if not is_first(it):
                            act.wait_ge(down_done, unit(it, j, UNITS - 1) - UNITS * U)
                        nc.scalar.activation(x_high[j][:], xT[j][:], ACT.Copy).then_inc(x_high_ready, 1)
                        nc.scalar.activation(c_parts[j][:], coefs[j][:], ACT.Copy).then_inc(c_high_ready, 1)
                    for j in range(U):
                        for u in range(UNITS + 1):
                            if u < UNITS:
                                i, b = pos(j, u) % 2, pos(j, u) % NB
                                act.wait_ge(guc_ready, unit(it, j, u))
                                after(act, h_ready, it, j, u, NB)
                                nc.scalar.activation(gated[b][:], ps_g[i][:], ACT.Silu, scale=1.0 / W_SCALE).then_inc(silu_ready, 1)
                            if u:
                                b = pos(j, u - 1) % NB
                                act.wait_ge(h_ready, unit(it, j, u - 1))
                                after(act, down_done, it, j, u - 1, NB)
                                nc.scalar.activation(h_high[b][:], hidden[b][:], ACT.Copy).then_inc(h_high_ready, 1)
                            if j and u == TAIL:
                                copy_out(it, j - 1)
                        if j == U - 1:
                            copy_out(it, j)

                def copy_out(it, j):
                    act.wait_ge(down_done, unit(it, j, UNITS - 1))
                    nc.scalar.activation(oT[j][:], ps_o[j][:], ACT.Copy, scale=1.0 / (W_SCALE * H_SCALE)).then_inc(oT_copied, 1)
                peeled(nc.scalar, steps, body)

            @block.vector
            def _(dve):
                own = Own(dve, dve_own)

                def low(it, j, u):
                    b = pos(j, u) % NB
                    dve.wait_ge(h_high_ready, unit(it, j, u))
                    nc.vector.tensor_tensor(h_low[b][:], hidden[b][:], h_high[b][:], ALU.subtract).then_inc(h_low_ready, 1)

                def tail(it, j):
                    dve.wait_ge(turned, nth(it, j))
                    nc.vector.tensor_tensor(y[j][:], ps_o[j][:].rearrange("p (q d) -> p q d", q=QT), x_sb[j][:], ALU.add).then_inc(x_added, 1)
                    dve.wait_ge(x_added, nth(it, j))
                    for q in range(QT):
                        m = own.mark(nc.vector.bn_stats(bn[j][:, q, :], y[j][:, q, :]))
                    own.wait(m)
                    dve.sem_inc(waited, 1)
                    for q in range(QT):
                        m = own.mark(nc.vector.bn_aggr(mv[j][:, q, :], bn[j][:, q, :]))
                    own.wait(m)
                    nc.vector.tensor_scalar(var_eps[j][:], mv[j][:, :, 1], EPS_OUT, None, ALU.add).then_inc(var_ready, 1)
                    dve.wait_ge(rstd_ready, nth(it, j))
                    if not is_first(it):
                        dve.wait_ge(stored[j], 16 * it)
                    for q in range(QT):
                        last = nc.vector.tensor_scalar(res[j][:, q, :], y[j][:, q, :], mv[j][:, q, 0:1], rstd[j][:, q:q + 1], ALU.subtract, ALU.mult)
                    last.then_inc(y_ready, 1)

                def body(it):
                    own.step(it)
                    for j in range(U):
                        for u in range(UNITS + 1):
                            if u < UNITS:
                                i, b = pos(j, u) % 2, pos(j, u) % NB
                                dve.wait_ge(silu_ready, unit(it, j, u))
                                after(dve, h_low_ready, it, j, u, NB)
                                if u < PAIRS_E:
                                    m = own.mark(nc.vector.tensor_tensor(gated[b][:], gated[b][:], ps_u[i][:], ALU.mult))
                                    own.wait(m)
                                    nc.vector.tensor_tensor(hidden[b][:], gated[b][:], ps_c[i][:], ALU.mult).then_inc(h_ready, 1)
                                else:
                                    nc.vector.scalar_tensor_tensor(hidden[b][:], ps_u[i][:], 1.0 / H_SCALE, gated[b][:], ALU.mult, ALU.mult).then_inc(h_ready, 1)
                            if u:
                                low(it, j, u - 1)
                            if j and u == TAIL:
                                tail(it, j - 1)
                    tail(it, U - 1)
                peeled(nc.vector, steps, body)


def program(nc, d, out):
    def dram(name, *shape):
        return nc.dram_tensor(name, shape, F32).ap()

    def inputs(block):
        return {k[len(block) + 1:]: v for k, v in d.items() if k.startswith(block + "_")}

    y1, x1, x3, x4, x5 = (dram(name, TOK, D) for name in ("y1", "x1", "x3", "x4", "x5"))
    x5T, coefT = dram("x5T", D, TOK), dram("coefT", 64, TOK)
    with Phase(nc, "all") as top:
        ident = make_ident(nc, top)
        with Phase(nc, "w0") as ph:
            w = setup_l0(nc, ph, inputs("attn0"), ident)
            with Phase(nc, "parts") as parts:
                xT_parts = [parts.sb(f"xT_{part}", [D, TOK], F16) for part in ("high", "low")]
                phase_max(nc, d["xT"], w["Wkp"], w, xT_parts)
                phase_performer(nc, w, d["x"], xT_parts, y1)
            phase_feed_forward0(nc, w, d["x"], y1, x1)
        with Phase(nc, "w2") as ph:
            w = setup_cross0(nc, ph, inputs("cross0"), ident)
            phase_cross0(nc, w, x1, d["ctx"], d["ctxT"], x3)
        with Phase(nc, "w3") as ph:
            w = setup_attn1(nc, ph, inputs("attn1"), ident)
            phase_attn1(nc, w, x3, x4)
        with Phase(nc, "w4") as ph:
            w = setup_cross1(nc, ph, inputs("cross1"), ident)
            phase_cross1(nc, w, x4, d["ctx"], d["ctxT"], x5, x5T)
            phase_router(nc, w, x5T, coefT)
        with Phase(nc, "w5") as ph:
            w = setup_moe(nc, ph, inputs("moe"), ident)
            phase_moe(nc, w, x5, x5T, coefT, out)


def kernel(**inputs):
    import numpy as np
    import concourse.bacc as bacc
    from concourse.bass_utils import run_bass_kernel_spmd

    a = {k: np.asarray(v) for k, v in inputs.items()}

    def layer(prefix):
        return {k[len(prefix) + 1:]: v for k, v in a.items() if k.startswith(prefix + "_")}

    def headed(m):
        return m.reshape(8, H, D).transpose(2, 1, 0).reshape(D, D)

    def side_by_side(experts, shared):
        return np.concatenate([experts.reshape(PAIRS_E, 2, D, 64).transpose(2, 0, 1, 3).reshape(D, PAIRS_E, P), shared[:, None, :]], 1)

    x, ctx = a["x"].reshape(TOK, D), a["ctx_1024"].reshape(TOK, D)
    head, row = np.arange(H), np.arange(P)
    arrays = dict(x=x, xT=x.T, ctx=ctx, ctxT=ctx.T)

    g = layer("L0_attn")
    q8 = {k: g[k].reshape(D, 8, P) for k in ("Wq", "Wk", "Wv")}
    attn0 = dict(q8, WqT=q8["Wq"].transpose(2, 1, 0), WkT=q8["Wk"].transpose(2, 1, 0), Wo=g["Wo"].reshape(8, P, D).transpose(1, 0, 2),
                 W1=g["W1"], W2=g["W2"].reshape(4, P, D).transpose(1, 0, 2), b1=g["b1"].reshape(1, 4 * P), b2=g["b2"].reshape(1, D),
                 projT=g["proj"].T, low_row=np.array([[0], [1]], np.float32), **{k: g[k].reshape(1, D) for k in ("ln1_g", "ln1_b", "ln2_g", "ln2_b")})

    g, f = layer("L0_xattn"), layer("L0_ffn")
    w1, w2, w3 = g["w_sim"].reshape(3, D, 1)
    cross0 = dict(Wqv=g["W_qv"].reshape(4, D, D).transpose(1, 0, 2), w1=w1, w2=w2, w3=w3, b_sim=g["b_sim"].reshape(1, 1),
                  b_qv=g["b_qv"].reshape(1, D), packed=f["packed_weight"].reshape(32, D).T,
                  ternary_scale=f["weight_scale"].reshape(1, 1), ffn_bias=f["bias"].reshape(1, D))

    g = layer("L1_attn")
    attn1 = dict(qkv_w=np.stack([g["q_w"], g["k_w"], g["v_w"]], 1), qkv_b=np.stack([g["q_b"], g["k_b"], g["v_b"]])[None],
                 out_w=g["out_w"], out_b=g["out_b"].reshape(1, D), bias_kT=g["bias_k"].reshape(H, 8).T,
                 bias_vT=g["bias_v"].reshape(H, 8).T, grep_w=g["grep_w"], grep_b=g["grep_b"].reshape(1, 8),
                 grep_a=g["grep_a"].reshape(1, H), rel_emb=g["rel_emb"],
                 quarter=(row[:, None] // 32 == np.arange(4)[None]).astype(np.float32),
                 nth_in_quarter=(head[:, None] % 4 == np.arange(4)[None]).astype(np.float32),
                 high_slot=(row[:, None] // 8 % 4 % 2 == 0).astype(np.float32), low_slot=(row[:, None] // 8 % 4 == 1).astype(np.float32),
                 own_head=np.eye(H, dtype=np.float32), down32=np.eye(P, k=-32, dtype=np.float32),
                 onehot=(np.arange(32)[:, None] == relative_buckets(np.arange(-127, 129))[None]).astype(np.float32))

    g, f = layer("L1_xattn"), layer("L1_ffn")
    cross1 = dict(Wq=headed(g["Wq"]), Wk=headed(g["Wk"]), Wo=g["Wo"].reshape(D, 8, H).transpose(2, 1, 0).reshape(D, D),
                  variant=((row[:, None] // 8) % 4 == np.arange(4)[None]).astype(np.float32),
                  router=f["router_w"].T, e_bias=f["e_bias"].reshape(1, 64))

    part_row, nth_pair, half = np.arange(64)[:, None, None], np.arange(16)[None, :, None], row[None, None, :] // 64
    moe = dict(Wg=side_by_side(f["Wg"], f["SWg"]), Wu=side_by_side(f["Wu"], f["SWu"]),
               Wd=np.concatenate([f["Wd"].reshape(PAIRS_E, P, D).transpose(1, 0, 2), f["SWd"][:, None, :]], 1),
               pick=(part_row % 32 == 2 * nth_pair + half).astype(np.float32))

    for name, block in (("attn0", attn0), ("cross0", cross0), ("attn1", attn1), ("cross1", cross1), ("moe", moe)):
        arrays.update({f"{name}_{k}": v for k, v in block.items()})
    arrays = {k: np.ascontiguousarray(v) for k, v in arrays.items()}

    nc = bacc.Bacc("TRN2", target_bir_lowering=False, num_devices=1)
    d = {k: nc.dram_tensor("in_" + k, v.shape, mybir.dt.from_np(v.dtype), kind="ExternalInput").ap() for k, v in arrays.items()}
    out = nc.dram_tensor("out", (TOK, D), F32, kind="ExternalOutput").ap()
    program(nc, d, out)
    done = run_bass_kernel_spmd(nc, [{"in_" + k: v for k, v in arrays.items()}], core_ids=[0])
    return done.results[0]["out"].reshape(B, S, D)
```
